# Optimizing a Trainium2 kernel written in Bass

```python
import numpy as np
import jax
import jax.numpy as jnp

def _softmax(x, axis=-1):
    return jax.nn.softmax(x, axis=axis)

def _gelu(x):
    return jax.nn.gelu(x, approximate=True)

def _silu(x):
    return jax.nn.silu(x)

def _sigmoid(x):
    return jax.nn.sigmoid(x)

def _layernorm(x, axis=-1, eps=1e-05):
    m = jnp.mean(x, axis=axis, keepdims=True)
    v = jnp.var(x, axis=axis, keepdims=True)
    return (x - m) / jnp.sqrt(v + eps)

def _scatter_add(tgt, idx, src, axis=0):
    return tgt.at[idx].add(src)

def _segment_sum(src, seg, n):
    return jax.ops.segment_sum(src, seg, n)
kernel_name = 'mk_hybrid_d1_jaxref_r8_827d92'

def setup_inputs(seed: int=0):
    np.random.seed(seed)
    _w = jnp.asarray

    def _L0_attn_a_setup():
        import jax, jax.numpy as jnp
        import numpy as np
        import math
        D_MODEL = 128
        N_HEADS = 16
        LATENT = 32
        key = jax.random.key(seed)
        ks = jax.random.split(key, 9)
        B, T, C, L = (2, 256, D_MODEL, LATENT)
        s = 0.02
        return {'x': jax.random.normal(ks[0], (B, T, C), dtype=jnp.float32), 'Wq': jax.random.normal(ks[1], (C, C), dtype=jnp.float32) * s, 'bq': jnp.zeros((C,), dtype=jnp.float32), 'Wkd': jax.random.normal(ks[2], (C, 2 * L), dtype=jnp.float32) * s, 'bkd': jnp.zeros((2 * L,), dtype=jnp.float32), 'Wku': jax.random.normal(ks[3], (L, 2 * C), dtype=jnp.float32) * s, 'bku': jnp.zeros((2 * C,), dtype=jnp.float32), 'Wo': jax.random.normal(ks[4], (C, C), dtype=jnp.float32) * s, 'bo': jnp.zeros((C,), dtype=jnp.float32)}
    _L0_attn_a_in = _L0_attn_a_setup()

    def _L0_attn_b_setup():
        import jax, jax.numpy as jnp
        import numpy as np
        import math
        B, S, D = (4, 256, 128)
        H = 16
        HD = D // H
        DL = 32
        LAMBDA_DECAY = 0.01
        key = jax.random.key(seed)
        ks = jax.random.split(key, 8)
        sc = lambda fan_in: 1.0 / math.sqrt(fan_in)
        return {'x': jax.random.normal(ks[0], (B, S, D), dtype=jnp.float32), 'W_q': jax.random.normal(ks[1], (D, D), dtype=jnp.float32) * sc(D), 'W_k': jax.random.normal(ks[2], (D, D), dtype=jnp.float32) * sc(D), 'W_v': jax.random.normal(ks[3], (D, D), dtype=jnp.float32) * sc(D), 'W_o': jax.random.normal(ks[4], (D, D), dtype=jnp.float32) * sc(D), 'W_down_kv': jax.random.normal(ks[5], (D, DL), dtype=jnp.float32) * sc(D), 'W_up_k': jax.random.normal(ks[6], (DL, D), dtype=jnp.float32) * sc(DL), 'W_up_v': jax.random.normal(ks[7], (DL, D), dtype=jnp.float32) * sc(DL)}
    _L0_attn_b_in = _L0_attn_b_setup()

    def _L0_ffn_setup():
        import jax, jax.numpy as jnp
        import numpy as np
        from jax import lax
        HIDDEN = 128
        INTER = 64
        E = 64
        K = 6
        G = 8
        TG = 4
        NSH = 2
        ISH = INTER * NSH

        def _moe_forward(hidden_states, gate_w, gate_bias, eg_w, eu_w, ed_w, sg_w, su_w, sd_w):
            B, S, H = hidden_states.shape
            x = hidden_states.reshape(-1, H)
            T = x.shape[0]
            shared = jax.nn.silu(x @ sg_w.T) * (x @ su_w.T) @ sd_w.T
            logits = x @ gate_w.T
            scores = jax.nn.sigmoid(logits) + gate_bias
            group_scores = scores.reshape(T, G, E // G).max(axis=-1)
            _, sel_groups = lax.top_k(group_scores, TG)
            group_mask = jnp.zeros((T, G), scores.dtype).at[jnp.arange(T)[:, None], sel_groups].set(1.0)
            mask = jnp.repeat(group_mask, E // G, axis=1)
            masked_scores = scores * mask
            topk_w, topk_i = lax.top_k(masked_scores, K)
            topk_w = topk_w / (topk_w.sum(axis=-1, keepdims=True) + 1e-08)
            comb = jnp.zeros((T, E), x.dtype).at[jnp.arange(T)[:, None], topk_i].add(topk_w)
            h = jax.nn.silu(jnp.einsum('th,eih->eti', x, eg_w)) * jnp.einsum('th,eih->eti', x, eu_w)
            routed = jnp.einsum('eti,ehi,te->th', h, ed_w, comb)
            return (shared + routed).reshape(B, S, H)
        key = jax.random.key(seed)
        ks = jax.random.split(key, 9)
        s = 0.02
        return {'hidden_states': jax.random.normal(ks[0], (1, 128, HIDDEN), jnp.float32), 'gate_w': jax.random.normal(ks[1], (E, HIDDEN), jnp.float32) * s, 'gate_bias': jnp.zeros((E,), jnp.float32), 'eg_w': jax.random.normal(ks[2], (E, INTER, HIDDEN), jnp.float32) * s, 'eu_w': jax.random.normal(ks[3], (E, INTER, HIDDEN), jnp.float32) * s, 'ed_w': jax.random.normal(ks[4], (E, HIDDEN, INTER), jnp.float32) * s, 'sg_w': jax.random.normal(ks[5], (ISH, HIDDEN), jnp.float32) * s, 'su_w': jax.random.normal(ks[6], (ISH, HIDDEN), jnp.float32) * s, 'sd_w': jax.random.normal(ks[7], (HIDDEN, ISH), jnp.float32) * s}
    _L0_ffn_in = _L0_ffn_setup()
    _d = {'L0_attn_a_x': _L0_attn_a_in['x'], 'L0_attn_a_Wq': _L0_attn_a_in['Wq'], 'L0_attn_a_bq': _L0_attn_a_in['bq'], 'L0_attn_a_Wkd': _L0_attn_a_in['Wkd'], 'L0_attn_a_bkd': _L0_attn_a_in['bkd'], 'L0_attn_a_Wku': _L0_attn_a_in['Wku'], 'L0_attn_a_bku': _L0_attn_a_in['bku'], 'L0_attn_a_Wo': _L0_attn_a_in['Wo'], 'L0_attn_a_bo': _L0_attn_a_in['bo'], 'L0_attn_b_W_q': _L0_attn_b_in['W_q'], 'L0_attn_b_W_k': _L0_attn_b_in['W_k'], 'L0_attn_b_W_v': _L0_attn_b_in['W_v'], 'L0_attn_b_W_o': _L0_attn_b_in['W_o'], 'L0_attn_b_W_down_kv': _L0_attn_b_in['W_down_kv'], 'L0_attn_b_W_up_k': _L0_attn_b_in['W_up_k'], 'L0_attn_b_W_up_v': _L0_attn_b_in['W_up_v'], 'L0_ffn_gate_w': _L0_ffn_in['gate_w'], 'L0_ffn_gate_bias': _L0_ffn_in['gate_bias'], 'L0_ffn_eg_w': _L0_ffn_in['eg_w'], 'L0_ffn_eu_w': _L0_ffn_in['eu_w'], 'L0_ffn_ed_w': _L0_ffn_in['ed_w'], 'L0_ffn_sg_w': _L0_ffn_in['sg_w'], 'L0_ffn_su_w': _L0_ffn_in['su_w'], 'L0_ffn_sd_w': _L0_ffn_in['sd_w']}
    _x0 = _d['L0_attn_a_x']
    _d['L0_attn_a_x'] = jax.random.normal(jax.random.fold_in(jax.random.key(seed), 1), (2, 1024, 128), dtype=_x0.dtype)
    del _x0
    return _d

def reference(L0_attn_a_x, L0_attn_a_Wq, L0_attn_a_bq, L0_attn_a_Wkd, L0_attn_a_bkd, L0_attn_a_Wku, L0_attn_a_bku, L0_attn_a_Wo, L0_attn_a_bo, L0_attn_b_W_q, L0_attn_b_W_k, L0_attn_b_W_v, L0_attn_b_W_o, L0_attn_b_W_down_kv, L0_attn_b_W_up_k, L0_attn_b_W_up_v, L0_ffn_gate_w, L0_ffn_gate_bias, L0_ffn_eg_w, L0_ffn_eu_w, L0_ffn_ed_w, L0_ffn_sg_w, L0_ffn_su_w, L0_ffn_sd_w):

    def _L0_attn_a_ref(x, Wq, bq, Wkd, bkd, Wku, bku, Wo, bo):
        import jax, jax.numpy as jnp
        import numpy as np
        import math
        D_MODEL = 128
        N_HEADS = 16
        LATENT = 32
        B, T, C = x.shape
        H = N_HEADS
        D = C // H
        L = LATENT
        q = (x @ Wq + bq).reshape(B, T, H, D)
        kv_latent = jax.nn.gelu(x @ Wkd + bkd, approximate=False)
        lat = kv_latent[..., :L] + kv_latent[..., L:]
        kv = lat @ Wku + bku
        k = kv[..., :C].reshape(B, T, H, D)
        v = kv[..., C:].reshape(B, T, H, D)
        scale = 1.0 / math.sqrt(D)
        attn = jnp.einsum('bqhd,bkhd->bhqk', q, k) * scale
        causal = jnp.tril(jnp.ones((T, T), dtype=bool))
        attn = jnp.where(causal, attn, -jnp.inf)
        attn = jax.nn.softmax(attn, axis=-1)
        out = jnp.einsum('bhqk,bkhd->bqhd', attn, v).reshape(B, T, C)
        return out @ Wo + bo

    def _L0_attn_b_ref(x, W_q, W_k, W_v, W_o, W_down_kv, W_up_k, W_up_v):
        import jax, jax.numpy as jnp
        import numpy as np
        import math
        B, S, D = (4, 256, 128)
        H = 16
        HD = D // H
        DL = 32
        LAMBDA_DECAY = 0.01
        b, s, d = x.shape
        q = x @ W_q
        k = x @ W_k
        v = x @ W_v
        latent_kv = (k + v) @ W_down_kv
        k_rec = (latent_kv @ W_up_k).reshape(b, s, H, HD).transpose(0, 2, 1, 3)
        v_rec = (latent_kv @ W_up_v).reshape(b, s, H, HD).transpose(0, 2, 1, 3)
        qh = q.reshape(b, s, H, HD).transpose(0, 2, 1, 3)
        scores = jnp.einsum('bhqd,bhkd->bhqk', qh, k_rec) / math.sqrt(d)
        t = jnp.arange(s, dtype=jnp.float32)
        decay = jnp.exp(-LAMBDA_DECAY * jnp.abs(t[:, None] - t[None, :]))
        scores = scores * decay[None, None, :, :]
        attn = jax.nn.softmax(scores, axis=-1)
        out = jnp.einsum('bhqk,bhkd->bhqd', attn, v_rec)
        out = out.transpose(0, 2, 1, 3).reshape(b, s, d)
        return out @ W_o

    def _L0_ffn_ref(hidden_states, gate_w, gate_bias, eg_w, eu_w, ed_w, sg_w, su_w, sd_w):
        import jax, jax.numpy as jnp
        import numpy as np
        from jax import lax
        HIDDEN = 128
        INTER = 64
        E = 64
        K = 6
        G = 8
        TG = 4
        NSH = 2
        ISH = INTER * NSH

        def _moe_forward(hidden_states, gate_w, gate_bias, eg_w, eu_w, ed_w, sg_w, su_w, sd_w):
            B, S, H = hidden_states.shape
            x = hidden_states.reshape(-1, H)
            T = x.shape[0]
            shared = jax.nn.silu(x @ sg_w.T) * (x @ su_w.T) @ sd_w.T
            logits = x @ gate_w.T
            scores = jax.nn.sigmoid(logits) + gate_bias
            group_scores = scores.reshape(T, G, E // G).max(axis=-1)
            _, sel_groups = lax.top_k(group_scores, TG)
            group_mask = jnp.zeros((T, G), scores.dtype).at[jnp.arange(T)[:, None], sel_groups].set(1.0)
            mask = jnp.repeat(group_mask, E // G, axis=1)
            masked_scores = scores * mask
            topk_w, topk_i = lax.top_k(masked_scores, K)
            topk_w = topk_w / (topk_w.sum(axis=-1, keepdims=True) + 1e-08)
            comb = jnp.zeros((T, E), x.dtype).at[jnp.arange(T)[:, None], topk_i].add(topk_w)
            h = jax.nn.silu(jnp.einsum('th,eih->eti', x, eg_w)) * jnp.einsum('th,eih->eti', x, eu_w)
            routed = jnp.einsum('eti,ehi,te->th', h, ed_w, comb)
            return (shared + routed).reshape(B, S, H)
        return _moe_forward(hidden_states, gate_w, gate_bias, eg_w, eu_w, ed_w, sg_w, su_w, sd_w)
    x = L0_attn_a_x
    x = x + _L0_attn_a_ref(_layernorm(x, axis=-1), L0_attn_a_Wq, L0_attn_a_bq, L0_attn_a_Wkd, L0_attn_a_bkd, L0_attn_a_Wku, L0_attn_a_bku, L0_attn_a_Wo, L0_attn_a_bo)
    x = x + _L0_ffn_ref(_layernorm(x, axis=-1), L0_ffn_gate_w, L0_ffn_gate_bias, L0_ffn_eg_w, L0_ffn_eu_w, L0_ffn_ed_w, L0_ffn_sg_w, L0_ffn_su_w, L0_ffn_sd_w)
    x = x + _L0_attn_b_ref(_layernorm(x, axis=-1), L0_attn_b_W_q, L0_attn_b_W_k, L0_attn_b_W_v, L0_attn_b_W_o, L0_attn_b_W_down_kv, L0_attn_b_W_up_k, L0_attn_b_W_up_v)
    x = x + _L0_ffn_ref(_layernorm(x, axis=-1), L0_ffn_gate_w, L0_ffn_gate_bias, L0_ffn_eg_w, L0_ffn_eu_w, L0_ffn_ed_w, L0_ffn_sg_w, L0_ffn_su_w, L0_ffn_sd_w)
    return x

_drawn_inputs = setup_inputs


def setup_inputs(seed=0):
    import zlib

    import numpy as np

    out = dict(_drawn_inputs(seed))
    spreads = {'L0_attn_a_bq': (0.0, 0.8),
     'L0_attn_a_bkd': (0.0, 0.8),
     'L0_attn_a_bku': (0.0, 0.1),
     'L0_attn_a_bo': (0.0, 0.1),
     'L0_ffn_gate_bias': (0.0, 0.8)}
    factors = {'L0_attn_a_Wq': 8.0,
     'L0_attn_a_Wkd': 8.0,
     'L0_attn_a_Wku': 8.0,
     'L0_attn_b_W_q': 2.729,
     'L0_attn_b_W_up_k': 2.731,
     'L0_ffn_gate_w': 8.0,
     'L0_ffn_eg_w': 8.0,
     'L0_ffn_eu_w': 8.0,
     'L0_ffn_ed_w': 8.0,
     'L0_ffn_sg_w': 4.962,
     'L0_ffn_su_w': 4.944,
     'L0_ffn_sd_w': 4.903}
    for name, (base, spread) in spreads.items():
        noise = np.random.default_rng([zlib.crc32(name.encode()), seed]).standard_normal(out[name].shape)
        drawn = base * np.exp(spread * noise) if base else spread * noise
        out[name] = jnp.asarray(drawn.astype(out[name].dtype))
    for name, factor in factors.items():
        out[name] = (out[name] * factor).astype(out[name].dtype)
    return out
```

```python
from contextlib import ExitStack, nullcontext

import concourse.bass as bass
from concourse import mybir

F32 = mybir.dt.float32
BF16 = mybir.dt.bfloat16
F16 = mybir.dt.float16
ALU = mybir.AluOpType
ACT = mybir.ActivationFunctionType
AX = mybir.AxisListType

P = 128
B, T, C, H = 2, 1024, 128, 16
D = C // H
TOK = B * T
NT = TOK // P
KT = T // P
HG = 4
NG = B * H // HG
BANK = 512
CH = TOK // BANK
TERMS = ((0, 1), (0, 0), (0, 2), (1, 0), (1, 1), (2, 0))
ROWS = len(TERMS) * D
MROW = 64
E, I, TOPK, GROUPS, TOPG = 64, 64, 6, 8, 4
PAIRS = E // 2
EPS = 1e-5
LAT = 32
XS, WS, HS = 16.0, 256.0, 16.0


def score_units(decayed):
    units = []
    for i in range(KT):
        if decayed:
            for h in range(HG):
                for half in range(2):
                    k0, k1, mid = half * BANK, (half + 1) * BANK, (i + 1) * P
                    pieces = []
                    if k0 < mid:
                        pieces.append((h, i, k0, min(k1, mid), 0, 0))
                    if mid < k1:
                        pieces.append((h, i, max(k0, mid), k1, max(k0, mid) - k0, 1))
                    diagonal = i * P - k0 if i // 4 == half else None
                    units.append((pieces, [], (h, 1, i, half, BANK, diagonal)))
            continue
        for half in range(1 + i // 4):
            k0, k1 = half * BANK, min((i + 1) * P, (half + 1) * BANK)
            n = k1 - k0
            per = BANK // n
            for h0 in range(0, HG, per):
                pieces = [(h0 + a, i, k0, k1, a * n, 0) for a in range(per)]
                masked = [(a + 1) * n - P for a in range(per)] if k1 == (i + 1) * P else []
                units.append((pieces, masked, (h0, per, i, half, n, None)))
    return units


def key_banks(decayed):
    def seg(j, half, col):
        q0 = max(j * P, half * BANK)
        return (0, j, q0, (half + 1) * BANK, col, col if q0 == j * P else None)
    low = [[seg(0, 0, 0)], [seg(0, 1, 0)], [seg(1, 1, 0)], [seg(2, 1, 0)], [seg(3, 1, 0)], [seg(4, 1, 0)],
           [seg(1, 0, 0), seg(3, 0, 384)], [seg(2, 0, 0), seg(6, 1, 256)], [seg(5, 1, 0), seg(7, 1, 384)]]
    if not decayed:
        return low
    high = []
    for bank in low:
        segs = []
        for (_, j, q0, q1, col, diag) in bank:
            jj, a, b = KT - 1 - j, T - q1, T - q0
            segs.append((1, jj, a, b, col, None if diag is None else col + (b - a) - P))
        high.append(segs)
    return low + high


def kernel_program(nc, ins, out):
    ctx = ExitStack()
    uid = [0]

    def name(s):
        uid[0] += 1
        return f"{s}_{uid[0]}"

    sems, phase_number = {}, [0]

    def sem(s):
        key = (phase_number[0], s)
        if key not in sems:
            sems[key] = ctx.enter_context(nc.semaphore(f"{s}_{phase_number[0]}"))
        return nullcontext(sems[key])

    def next_phase():
        phase_number[0] += 1

    with ctx:
        def keep(s, shape, dt):
            return ctx.enter_context(nc.sbuf_tensor(s, shape, dt))

        ps = ctx.enter_context(nc.psum_tensor("ps", [P, 8 * BANK], F32))

        def bank(i, n=1):
            return ps[:, i * BANK:(i + n) * BANK]

        x_tok = keep("x_tok", [P, NT, C], F32)
        attn_tok = keep("attn_tok", [P, NG, KT, HG, D], F32)
        v_aug = keep("v_aug", [P, NG, KT, HG, 32], F32)
        s_stack = [keep(f"s_{o}", [P, 2, HG, T], BF16) for o in "qk"]
        t_stack = [[keep(f"t_{o}_{b}", [P, 2, HG, T], BF16) for o in "qk"] for b in range(2)]
        ident = keep("ident", [P, P], F32)
        ident_b = keep("ident_b", [P, P], BF16)
        scratch = [nc.dram_tensor(f"parts_{o}", [NG, HG, D, len(TERMS), 2, T], BF16, kind="Internal").ap() for o in "qk"]
        start_phase(nc, sem, ins, x_tok, ident, ident_b, v_aug, s_stack, t_stack)
        for layer in range(2):
            if layer == 1:
                clear_semaphores(nc, [s for (number, _), s in sems.items() if number >= 1])
            phase_number[0] = 1
            with ExitStack() as phase:
                def sb(s, shape, dt):
                    return phase.enter_context(nc.sbuf_tensor(name(s), shape, dt))
                xnT = sb("xnT", [P, TOK], F32)
                norm_phase(nc, sem, name, x_tok, ident, xnT, None, bank)
                next_phase()
                if layer == 0:
                    project_first(nc, sem, sb, ins, xnT, v_aug, scratch, bank)
                else:
                    project_second(nc, sem, sb, ins, xnT, v_aug, scratch, bank)
            with ExitStack() as phase:
                def sb(s, shape, dt):
                    return phase.enter_context(nc.sbuf_tensor(name(s), shape, dt))
                next_phase()
                attention_phase(nc, sem, sb, ins, layer == 1, v_aug, scratch, s_stack, t_stack, ident, ident_b,
                                attn_tok, bank)
            with ExitStack() as phase:
                def sb(s, shape, dt):
                    return phase.enter_context(nc.sbuf_tensor(name(s), shape, dt))
                next_phase()
                output_phase(nc, sem, sb, ins, layer, attn_tok, x_tok, ident, bank)
            with ExitStack() as phase:
                def sb(s, shape, dt):
                    return phase.enter_context(nc.sbuf_tensor(name(s), shape, dt))
                xh = sb("xh", [P, TOK], F16)
                xl = sb("xl", [P, TOK], F16)
                comb = sb("comb", [96, 2, TOK], BF16)
                with ExitStack() as route:
                    def rb(s, shape, dt):
                        return route.enter_context(nc.sbuf_tensor(name(s), shape, dt))
                    xnT = rb("xnT", [P, TOK], F32)
                    next_phase()
                    norm_phase(nc, sem, name, x_tok, ident, xnT, (xh, xl), bank)
                    next_phase()
                    route_phase(nc, sem, rb, ins, xnT, comb, ident, bank)
                next_phase()
                expert_phase(nc, sem, sb, ins, xh, xl, comb, x_tok, ident, bank, out if layer == 1 else None)


def clear_semaphores(nc, sems):
    numbers = sorted(s.num for s in sems)
    assert numbers == list(range(numbers[0], numbers[-1] + 1))
    with nc.Block() as block:
        @block.sync
        def _(sp):
            sp.sem_clear(range(numbers[0], numbers[-1] + 1))


def start_phase(nc, sem, ins, x_tok, ident, ident_b, v_aug, s_stack, t_stack):
    with sem("x_loaded") as x_loaded, sem("zeroed") as zeroed, nc.Block() as block:
        @block.sync
        def _(sp):
            sp.dma_start(x_tok[:, :, :], ins["x"].rearrange("(t p) c -> p t c", p=P)).then_inc(x_loaded, 16)
            sp.dma_start(ident[:, :], ins["ident"]).then_inc(x_loaded, 16)
            sp.dma_start(ident_b[:, :], ins["ident_b"]).then_inc(x_loaded, 16)
            sp.wait_ge(x_loaded, 48)

        stacks = [side[:, v] for group in ([s_stack] + t_stack) for side in group for v in range(2)]
        ones = [t_stack[b][1][:, v] for b in range(2) for v in range(2)]

        @block.vector
        def _(dve):
            for s in stacks:
                last = nc.vector.memset(s[:, :, :], 0.0).then_inc(zeroed, 1)
            dve.wait_ge(zeroed, len(stacks))
            for s in ones:
                nc.vector.memset(s[MROW:MROW + 3, :, :], 1.0)

        @block.gpsimd
        def _(pool):
            nc.gpsimd.memset(v_aug[:, :, :, :, 0:8], 0.0)
            nc.gpsimd.memset(v_aug[:, :, :, :, 8:9], 1.0)
            nc.gpsimd.memset(v_aug[:, :, :, :, 9:32], 0.0)


def norm_phase(nc, sem, name, x_tok, ident, xnT, halves, bank):
    with ExitStack() as c:
        stats = c.enter_context(nc.sbuf_tensor(name("stats"), [P, NT, 6], F32))
        mv = c.enter_context(nc.sbuf_tensor(name("mv"), [P, NT, 2], F32))
        ve = c.enter_context(nc.sbuf_tensor(name("ve"), [P, 4, NT], F32))
        xn = c.enter_context(nc.sbuf_tensor(name("xn"), [P, NT, C], F32))
        stat_ready, var_ready, rstd_ready, shift_ready, xn_ready, turned, evacuated, high_ready = (
            c.enter_context(sem(s)) for s in ("stat_ready", "var_ready", "rstd_ready", "shift_ready", "xn_ready",
                                              "turned", "evacuated", "high_ready"))
        block = c.enter_context(nc.Block())

        @block.vector
        def _(dve):
            nc.vector.memset(ve[:, 1, :], -0.5)
            for t in range(NT):
                nc.vector.bn_stats(stats[:, t, :], x_tok[:, t, :]).then_inc(stat_ready, 1)
            for t in range(NT):
                dve.wait_ge(stat_ready, t + 1)
                nc.vector.bn_aggr(mv[:, t, :], stats[:, t, :]).then_inc(stat_ready, 1)
            dve.wait_ge(stat_ready, 2 * NT)
            nc.vector.tensor_scalar(ve[:, 0, :], mv[:, :, 1], EPS, None, ALU.add).then_inc(var_ready, 1)
            dve.wait_ge(rstd_ready, 1)
            nc.vector.scalar_tensor_tensor(out=ve[:, 3, :], in0=mv[:, :, 0], scalar=-1.0, in1=ve[:, 2, :],
                                           op0=ALU.mult, op1=ALU.mult).then_inc(shift_ready, 1)
            dve.wait_ge(shift_ready, 1)
            for t in range(NT):
                nc.vector.tensor_scalar(xn[:, t, :], x_tok[:, t, :], ve[:, 2, t:t + 1], ve[:, 3, t:t + 1],
                                        ALU.mult, ALU.add).then_inc(xn_ready, 1)
            if halves:
                for k in range(CH):
                    dve.wait_ge(high_ready, k + 1)
                    nc.vector.scalar_tensor_tensor(
                        out=halves[1][:, k * BANK:(k + 1) * BANK], in0=bank(k), scalar=XS,
                        in1=halves[0][:, k * BANK:(k + 1) * BANK], op0=ALU.mult, op1=ALU.subtract)

        @block.gpsimd
        def _(pool):
            pool.wait_ge(var_ready, 1)
            nc.gpsimd.tensor_tensor(ve[:, 2, :], ve[:, 0, :], ve[:, 1, :], ALU.pow).then_inc(rstd_ready, 1)

        @block.tensor
        def _(pe):
            for t in range(NT):
                pe.wait_ge(xn_ready, t + 1)
                nc.tensor.transpose(bank(t // 4)[:, t % 4 * P:(t % 4 + 1) * P], xn[:, t, :], ident[:, :])\
                    .then_inc(turned, 1)

        @block.scalar
        def _(act):
            for k in range(CH):
                act.wait_ge(turned, 4 * (k + 1))
                chunk = slice(k * BANK, (k + 1) * BANK)
                nc.scalar.activation(xnT[:, chunk], bank(k), ACT.Copy)
                if halves:
                    nc.scalar.activation(halves[0][:, chunk], bank(k), ACT.Copy, scale=XS).then_inc(high_ready, 1)


class SplitJobs:

    def __init__(self, nc, sem, sb, c, jobs, scratch):
        self.nc, self.jobs, self.scratch = nc, jobs, scratch
        self.value = sb("value", [P, 3, BANK], F32)
        self.rest = sb("rest", [P, 2, BANK], F32)
        self.parts = sb("parts", [P, 3, 3, BANK], BF16)
        self.value_ready, self.first_ready, self.rest_ready, self.second_ready, self.third_ready = (
            c.enter_context(sem(s)) for s in ("value_ready", "first_ready", "rest_ready", "second_ready",
                                              "third_ready"))
        self.stored = [c.enter_context(sem(f"stored{i}")) for i in range(3)]

    def vector(self, dve, make_value):
        nc, n = self.nc, len(self.jobs)
        for j in range(n + 1):
            if j < n:
                if j >= 3:
                    dve.wait_ge(self.rest_ready, j - 2)
                make_value(j, self.value[:, j % 3, :]).then_inc(self.value_ready, 1)
            if j >= 1:
                dve.wait_ge(self.first_ready, j)
                if j >= 3:
                    dve.wait_ge(self.third_ready, j - 2)
                a = (j - 1) % 2
                nc.vector.tensor_tensor(self.rest[:, a, :], self.value[:, (j - 1) % 3, :], self.parts[:, (j - 1) % 3, 0, :],
                                        ALU.subtract).then_inc(self.rest_ready, 1)

    def scalar(self, act):
        nc, n = self.nc, len(self.jobs)
        for j in range(n + 1):
            if j < n:
                act.wait_ge(self.value_ready, j + 1)
                if j >= 3:
                    act.wait_ge(self.stored[j % 3], 48 * (j // 3))
                nc.scalar.activation(self.parts[:, j % 3, 0, :], self.value[:, j % 3, :], ACT.Copy)\
                    .then_inc(self.first_ready, 1)
            if j >= 1:
                act.wait_ge(self.rest_ready, j)
                nc.scalar.activation(self.parts[:, (j - 1) % 3, 1, :], self.rest[:, (j - 1) % 2, :], ACT.Copy)\
                    .then_inc(self.second_ready, 1)

    def gpsimd(self, pool):
        for j in range(len(self.jobs)):
            pool.wait_ge(self.second_ready, j + 1)
            self.nc.gpsimd.tensor_tensor(self.parts[:, j % 3, 2, :], self.rest[:, j % 2, :],
                                         self.parts[:, j % 3, 1, :], ALU.subtract).then_inc(self.third_ready, 1)

    def sync(self, sp):
        for j, (operand, variant, k) in enumerate(self.jobs):
            sp.wait_ge(self.third_ready, j + 1)
            b, t0 = k * BANK // T, k * BANK % T
            for p in range(3):
                places = [r for r, term in enumerate(TERMS) if term[operand] == p]
                step = places[1] - places[0] if len(places) > 1 else 1
                to = self.scratch[operand][b * HG:(b + 1) * HG, :, :, places[0]:places[-1] + 1:step, variant,
                                           t0:t0 + BANK].rearrange("g h d m t -> (g h d) m t")
                part = self.parts[:, j % 3, p, :].rearrange("p (o t) -> p o t", o=1)
                sp.dma_start(to, part.broadcast_to([P, len(places), BANK])).then_inc(self.stored[j % 3], 16)
        for i in range(3):
            sp.wait_ge(self.stored[i], 48 * len([j for j in range(len(self.jobs)) if j % 3 == i]))


def v_slot(v_aug, t):
    b, j = divmod(t, KT)
    return v_aug[:, b * HG:(b + 1) * HG, j, :, 0:D]


def project_first(nc, sem, sb, ins, xnT, v_aug, scratch, bank):
    wq = sb("wq", [P, C], F32)
    wkd = sb("wkd", [P, 2 * LAT], F32)
    wku = sb("wku", [2 * LAT, 2 * C], F32)
    bq = sb("bq", [P, 1], F32)
    bkd = sb("bkd", [2 * LAT, 1], F32)
    bk = sb("bk", [P, 1], F32)
    bv = sb("bv", [P, C], F32)
    latent = sb("latent", [2 * LAT, TOK], F32)
    with ExitStack() as c:
        loaded, latent_ps, latent_ready, qk_ps, v_ps, v_taken = (
            c.enter_context(sem(s)) for s in ("loaded", "latent_ps", "latent_ready", "qk_ps", "v_ps", "v_taken"))
        jobs = [(o, 0, k) for k in range(CH) for o in range(2)]
        split = SplitJobs(nc, sem, sb, c, jobs, scratch)
        block = c.enter_context(nc.Block())

        @block.sync
        def _(sp):
            bku = ins["bku"]
            for dst, src in ((wq[:, :], ins["wq"]), (wkd[:, :], ins["wkd"]), (wku[0:LAT, :], ins["wku"]),
                             (wku[LAT:2 * LAT, :], ins["wku"]), (bq[:, :], ins["bq"].rearrange("(p o) -> p o", o=1)),
                             (bkd[:, :], ins["bkd"].rearrange("(p o) -> p o", o=1)),
                             (bk[:, :], bku[0:C].rearrange("(p o) -> p o", o=1)),
                             (bv[:, :], bku[C:2 * C].rearrange("(o n) -> o n", o=1).broadcast_to([P, C]))):
                sp.dma_start(dst, src).then_inc(loaded, 16)
            split.sync(sp)

        @block.tensor
        def _(pe):
            pe.wait_ge(loaded, 8 * 16)
            for k in range(CH):
                nc.tensor.matmul(bank(k)[0:2 * LAT, :], wkd[:, :], xnT[:, k * BANK:(k + 1) * BANK],
                                 start=True, stop=True).then_inc(latent_ps, 1)
            for j, (o, _, k) in enumerate(jobs):
                chunk = slice(k * BANK, (k + 1) * BANK)
                if j >= 2:
                    pe.wait_ge(split.value_ready, j - 1)
                if o == 0:
                    nc.tensor.matmul(bank(4 + j % 2), wq[:, :], xnT[:, chunk], start=True, stop=True)\
                        .then_inc(qk_ps, 1)
                else:
                    pe.wait_ge(latent_ready, k + 1)
                    nc.tensor.matmul(bank(4 + j % 2), wku[:, 0:C], latent[:, chunk], start=True, stop=True)\
                        .then_inc(qk_ps, 1)
            for k in range(CH):
                if k >= 2:
                    pe.wait_ge(v_taken, 4 * (k - 1))
                for t in range(4 * k, 4 * k + 4):
                    nc.tensor.matmul(bank(6 + k % 2)[:, t % 4 * P:(t % 4 + 1) * P], latent[:, t * P:(t + 1) * P],
                                     wku[:, C:2 * C], start=True, stop=True).then_inc(v_ps, 1)

        @block.scalar
        def _(act):
            act.wait_ge(loaded, 8 * 16)
            for k in range(CH):
                act.wait_ge(latent_ps, k + 1)
                nc.scalar.activation(latent[:, k * BANK:(k + 1) * BANK], bank(k)[0:2 * LAT, :], ACT.Gelu,
                                     bias=bkd[:, 0:1]).then_inc(latent_ready, 1)
            split.scalar(act)

        @block.gpsimd
        def _(pool):
            split.gpsimd(pool)

        @block.vector
        def _(dve):
            dve.wait_ge(loaded, 8 * 16)

            def value(j, dst):
                dve.wait_ge(qk_ps, j + 1)
                return nc.vector.tensor_scalar(dst, bank(4 + j % 2), (bq, bk)[jobs[j][0]][:, 0:1], None, ALU.add)
            split.vector(dve, value)
            for t in range(NT):
                dve.wait_ge(v_ps, t // 4 * 4 + 4)
                src = bank(6 + t // 4 % 2)[:, t % 4 * P:(t % 4 + 1) * P].rearrange("p (g h d) -> p g h d", g=HG, d=D)
                nc.vector.tensor_tensor(v_slot(v_aug, t), src,
                                        bv[:, :].rearrange("p (g h d) -> p g h d", g=HG, d=D), ALU.add)\
                    .then_inc(v_taken, 1)


def project_second(nc, sem, sb, ins, xnT, v_aug, scratch, bank):
    wq = sb("wq", [P, C], F32)
    wk = sb("wk", [P, C], F32)
    wv = sb("wv", [P, C], F32)
    wd = sb("wd", [P, LAT], F32)
    wuk = sb("wuk", [LAT, C], F32)
    wuv = sb("wuv", [LAT, C], F32)
    decay = sb("decay", [P, 2, T], F32)
    kv = sb("kv", [P, TOK], F32)
    latent = sb("latent", [LAT, TOK], F32)
    with ExitStack() as c:
        loaded, kv_ps, kv_ready, latent_ps, latent_ready, qk_ps, v_ps, v_taken = (
            c.enter_context(sem(s)) for s in ("loaded", "kv_ps", "kv_ready", "latent_ps", "latent_ready", "qk_ps",
                                              "v_ps", "v_taken"))
        jobs = [(o, v, k) for k in range(CH) for o in range(2) for v in range(2)]
        split = SplitJobs(nc, sem, sb, c, jobs, scratch)
        block = c.enter_context(nc.Block())

        @block.sync
        def _(sp):
            for dst, src in ((wq, "b_wq"), (wk, "b_wk"), (wv, "b_wv"), (wd, "b_wd"), (wuk, "b_wuk"), (wuv, "b_wuv")):
                sp.dma_start(dst[:, :], ins[src]).then_inc(loaded, 16)
            for v in range(2):
                sp.dma_start(decay[:, v, :], ins["decay"][v:v + 1, :].broadcast_to([P, T])).then_inc(loaded, 16)
            split.sync(sp)

        @block.tensor
        def _(pe):
            pe.wait_ge(loaded, 8 * 16)
            for k in range(CH):
                chunk = slice(k * BANK, (k + 1) * BANK)
                nc.tensor.matmul(bank(k), wk[:, :], xnT[:, chunk], start=True, stop=False)
                nc.tensor.matmul(bank(k), wv[:, :], xnT[:, chunk], start=False, stop=True).then_inc(kv_ps, 1)
            for k in range(CH):
                chunk = slice(k * BANK, (k + 1) * BANK)
                pe.wait_ge(kv_ready, k + 1)
                nc.tensor.matmul(bank(k)[0:LAT, :], wd[:, :], kv[:, chunk], start=True, stop=True)\
                    .then_inc(latent_ps, 1)
            for m in range(2 * CH):
                k, o = divmod(m, 2)
                chunk = slice(k * BANK, (k + 1) * BANK)
                if m >= 2:
                    pe.wait_ge(split.value_ready, 2 * (m - 1))
                if o == 0:
                    nc.tensor.matmul(bank(4 + m % 2), wq[:, :], xnT[:, chunk], start=True, stop=True)\
                        .then_inc(qk_ps, 1)
                else:
                    pe.wait_ge(latent_ready, k + 1)
                    nc.tensor.matmul(bank(4 + m % 2), wuk[:, :], latent[:, chunk], start=True, stop=True)\
                        .then_inc(qk_ps, 1)
            for k in range(CH):
                if k >= 2:
                    pe.wait_ge(v_taken, 4 * (k - 1))
                for t in range(4 * k, 4 * k + 4):
                    nc.tensor.matmul(bank(6 + k % 2)[:, t % 4 * P:(t % 4 + 1) * P], latent[:, t * P:(t + 1) * P],
                                     wuv[:, :], start=True, stop=True).then_inc(v_ps, 1)

        @block.scalar
        def _(act):
            for k in range(CH):
                act.wait_ge(kv_ps, k + 1)
                nc.scalar.activation(kv[:, k * BANK:(k + 1) * BANK], bank(k), ACT.Copy).then_inc(kv_ready, 1)
            for k in range(CH):
                act.wait_ge(latent_ps, k + 1)
                nc.scalar.activation(latent[:, k * BANK:(k + 1) * BANK], bank(k)[0:LAT, :], ACT.Copy)\
                    .then_inc(latent_ready, 1)
            split.scalar(act)

        @block.gpsimd
        def _(pool):
            split.gpsimd(pool)

        @block.vector
        def _(dve):
            dve.wait_ge(loaded, 8 * 16)

            def value(j, dst):
                o, v, k = jobs[j]
                dve.wait_ge(qk_ps, j // 2 + 1)
                t0 = k * BANK % T
                factor = decay[:, v if o == 0 else 1 - v, t0:t0 + BANK]
                return nc.vector.tensor_tensor(dst, bank(4 + j // 2 % 2), factor, ALU.mult)
            split.vector(dve, value)
            for t in range(NT):
                dve.wait_ge(v_ps, t // 4 * 4 + 4)
                src = bank(6 + t // 4 % 2)[:, t % 4 * P:(t % 4 + 1) * P].rearrange("p (g h d) -> p g h d", g=HG, d=D)
                nc.vector.tensor_copy(v_slot(v_aug, t), src).then_inc(v_taken, 1)


def attention_phase(nc, sem, sb, ins, decayed, v_aug, scratch, s_stack, t_stack, ident, ident_b, attn_tok, bank):
    variants = range(2 if decayed else 1)
    units, banks = score_units(decayed), key_banks(decayed)
    steps = [banks[i:i + 2] for i in range(0, len(banks), 2)]
    NU, NS = len(units), len(steps)
    scale = (C if decayed else D) ** -0.5
    NV = len(variants)

    prob = sb("prob", [P, 2, HG, 2 * BANK], F32)
    v_group = sb("v_group", [P, 2, KT, HG, 32], F32)
    o_sum = sb("o_sum", [P, T], F32)
    half_max = sb("half_max", [P, HG, KT, 2], F32)
    row_max = sb("row_max", [P, HG, KT], F32)
    max_parts = sb("max_parts", [HG * KT, 3, P], BF16)
    max_rest = sb("max_rest", [HG * KT, P], F32)
    inverse = sb("inverse", [P, 2, 4, HG], F32)
    mask = sb("mask", [P, 3, P], BF16)
    if decayed:
        diagonal = sb("diagonal", [P, 7 * P], F32)
        junk = sb("junk", [P, BANK], BF16)
        spare = sb("spare", [P, 1], F32)

    def schedule(with_scores, with_norm):
        main = []
        for s in range(NS):
            main += [("ST", s, 0), ("ST", s, 1)]
            if s > 0:
                main += [("PV", s - 1, b) for b in range(len(steps[s - 1]))]
            elif with_norm:
                main += [("END", NS - 1, b) for b in range(len(steps[-1]))]
            main += [("ST", s, 2), ("ST", s, 3)]
            if s == 1 and with_norm:
                main += [("ON", 0, 0), ("ON", 1, 0)]
        if not with_scores:
            return main
        cost = {"ST": 4, "PV": 8, "END": 8, "ON": 4}
        whole = sum(cost[kind] for kind, _, _ in main)
        order, done, passed, turn = [], 0, 0, None
        for item in main:
            order.append(item)
            passed += cost[item[0]]
            if turn is not None and passed >= turn:
                order.append(("MT", 0, 0))
                turn = None
            upto = min(NU, int(NU * passed / (SPREAD * whole)))
            order += [("S", u, 0) for u in range(done, upto)]
            if done < NU <= upto:
                turn = passed + 8
            done = upto
        assert turn is None
        return order

    def slots_before(n):
        return NU + 1 if type(n) is int and n == 0 else (n - 1) * (NU + 3) + 2 * (NU + 1)

    def chain_before(n):
        return 2 if type(n) is int and n == 0 else (n - 1) * 4 + 4

    def last_slot(n, order, kind):
        kinds = [k for k, _, _ in order if k in ("S", "MT", "ON")]
        return slots_before(n) + (max(i for i, k in enumerate(kinds) if k == kind) + 1)

    SPREAD = 0.85
    prologue = [("S", u, 0) for u in range(NU)] + [("MT", 0, 0)]
    first, middle, final = schedule(True, False), schedule(True, True), schedule(False, True)
    closing = [("END", NS - 1, b) for b in range(len(steps[-1]))] + [("ON", 0, 0), ("ON", 1, 0)]

    def order_of(n):
        return first if type(n) is int and n == 0 else final if type(n) is int and n == NG - 1 else middle

    def iterations(eng, body):
        body(0, 0)
        with eng.Fori(1, NG - 1, 2) as i:
            body(i, 1)
            body(i + 1, 0)
        body(NG - 1, 1)

    with ExitStack() as c:
        t_loaded, v_loaded = ([c.enter_context(sem(f"{s}_loaded{b}")) for b in range(2)] for s in "tv")
        (const_loaded, s_loaded, m_loaded, slot_full, slot_free, st_full, exp_done, pv_done,
         o_ready, max_ready, parts_ready, vector_done, preset) = (
            c.enter_context(sem(s)) for s in (
                "const_loaded", "s_loaded", "m_loaded", "slot_full", "slot_free", "st_full",
                "exp_done", "pv_done", "o_ready", "max_ready", "parts_ready", "vector_done", "preset"))
        block = c.enter_context(nc.Block())

        @block.sync
        def _(sp):
            def stack_load(stack, n, loaded):
                for side in range(2):
                    src = scratch[side][bass.ds(n, 1)].rearrange("o h d m v t -> (o d m) v h t")
                    for v in variants:
                        sp.dma_start(stack[side][0:ROWS, v], src[:, v]).then_inc(loaded, 16)

            def values_load(n, par):
                sp.dma_start(v_group[:, par].rearrange("p k h m -> p (k h m)"),
                             v_aug[:, bass.ds(n, 1)].rearrange("p o k h m -> p (o k h m)")).then_inc(v_loaded[par], 16)

            def maxima_load(par):
                for v in variants:
                    for p in range(3):
                        sp.dma_start(t_stack[par][0][MROW + p:MROW + p + 1, v, :, :], max_parts[:, p, :])\
                            .then_inc(m_loaded, 16)

            def body(n, par, with_scores=True, before=None):
                first_one = type(n) is int and n == 0
                if not first_one:
                    sp.wait_ge(st_full, n * (4 * NS))
                stack_load(t_stack[1 - par], n + 1, t_loaded[1 - par])
                if not first_one:
                    sp.wait_ge(pv_done, n * NS)
                values_load(n + 1, 1 - par)
                if with_scores:
                    sp.wait_ge(slot_full, last_slot(n, order_of(n), "S"))
                    stack_load(s_stack, n + 2, s_loaded)
                sp.wait_ge(parts_ready, n + 2)
                maxima_load(1 - par)

            stack_load(s_stack, 0, s_loaded)
            sp.dma_start(mask[:, :, :], ins["mask"].rearrange("m p n -> p m n")).then_inc(const_loaded, 16)
            if decayed:
                sp.dma_start(diagonal[:, :], ins["diagonal"]).then_inc(const_loaded, 16)
            stack_load(t_stack[0], 0, t_loaded[0])
            values_load(0, 0)
            sp.wait_ge(slot_full, NU)
            stack_load(s_stack, 1, s_loaded)
            sp.wait_ge(parts_ready, 1)
            maxima_load(0)
            body(0, 0)
            with sp.Fori(1, NG - 3, 2) as i:
                body(i, 1)
                body(i + 1, 0)
            body(NG - 3, 1)
            body(NG - 2, 0, with_scores=False)

        @block.tensor
        def _(pe):
            pe.wait_ge(const_loaded, 32 if decayed else 16)

            def work(order, n, par, slot, target):
                base = slot
                parity = slot_parity(order, n)
                k = 0
                for kind, a, b in order:
                    if kind in ("S", "MT", "ON"):
                        at = bank((parity + k) % 2)
                        if not (type(base) is int and base + k < 2):
                            pe.wait_ge(slot_free, base + (k - 1))
                        k += 1
                    if kind == "S":
                        if a == 0:
                            pe.wait_ge(s_loaded, (target + 1) * (32 * NV))
                        pieces, masked, _ = units[a]
                        todo = []
                        for (h, i, k0, k1, col, v) in pieces:
                            todo.append((at[:, col:col + k1 - k0], s_stack[0][:, v, h, i * P:(i + 1) * P],
                                         s_stack[1][:, v, h, k0:k1], True, (k1 - k0 + col - P) not in masked))
                            if k1 - k0 + col - P in masked:
                                col = k1 - k0 + col - P
                                todo.append((at[:, col:col + P], ident_b[:, :], mask[:, 0, :], False, True))
                        for o, l, r, st, sp_ in todo:
                            last = nc.tensor.matmul(o, l, r, start=st, stop=sp_)
                        last.then_inc(slot_full, 1)
                    elif kind == "MT":
                        pe.wait_ge(max_ready, target + 1)
                        nc.tensor.transpose(at[0:HG * KT, 0:P], row_max[:, :, :].rearrange("p h k -> p (h k)"),
                                            ident[:, :]).then_inc(slot_full, 1)
                    elif kind == "ON":
                        if a == 0:
                            pe.wait_ge(o_ready, n * 2)
                        for q in range(4):
                            last = nc.tensor.transpose(at[:, q * P:(q + 1) * P],
                                                       o_sum[:, (4 * a + q) * P:(4 * a + q + 1) * P], ident[:, :])
                        last.then_inc(slot_full, 1)
                    elif kind == "ST":
                        if a == 0 and b == 0:
                            pe.wait_ge(t_loaded[par], (n + (2 - par)) * (16 * NV))
                            pe.wait_ge(m_loaded, (n + 1) * (48 * len(variants)))
                        t = 4 * a + b
                        if not (type(n) is int and n == 0 and t < 2):
                            pe.wait_ge(exp_done, n * (4 * NS) + (t - 1))
                        for x, segs in enumerate(steps[a]):
                            for (v, j, q0, q1, col, diag) in segs:
                                dst = bank(2 + 2 * (t % 2) + x)
                                last = nc.tensor.matmul(dst[:, col:col + q1 - q0],
                                                        t_stack[par][1][:, v, b, j * P:(j + 1) * P],
                                                        t_stack[par][0][:, v, b, q0:q1],
                                                        start=True, stop=diag is None)
                                if diag is not None:
                                    last = nc.tensor.matmul(dst[:, diag:diag + P], ident_b[:, :], mask[:, 1 + v, :],
                                                            start=False, stop=True)
                        last.then_inc(st_full, 1)
                    elif kind == "PV":
                        if a == 0 and b == 0:
                            pe.wait_ge(v_loaded[par], (n + (2 - par)) * 8)
                            if not (type(n) is int and n == 0):
                                pe.wait_ge(o_ready, n * 2)
                        if b == 0:
                            pe.wait_ge(exp_done, n * (4 * NS) + 4 * (a + 1))
                        product(a, b, par)
                    elif kind == "END":
                        if b == 0:
                            pe.wait_ge(exp_done, n * (4 * NS))
                        product(a, b, 1 - par)

            def product(a, b, par):
                for (v, j, q0, q1, col, _) in steps[a][b]:
                    half = q0 // BANK
                    ends = last_of_half[half] == (a, b, j)
                    for h in range(HG):
                        last = nc.tensor.matmul(
                            bank(6 + half)[32 * h:32 * h + 32, q0 - half * BANK:q1 - half * BANK],
                            v_group[:, par, j, h, :],
                            prob[:, (par + a) % 2, h, b * BANK + col:b * BANK + col + q1 - q0],
                            start=(a == 0), stop=ends, skip_group_check=True)
                if b == len(steps[a]) - 1:
                    last.then_inc(pv_done, 1)

            last_of_half = {}
            for a, st in enumerate(steps):
                for b, segs in enumerate(st):
                    for seg in segs:
                        last_of_half[seg[2] // BANK] = (a, b, seg[1])

            def slot_parity(order, n):
                if order is prologue:
                    return 0
                if order is closing:
                    return (slots_before(NG - 1) + 2) % 2
                if type(n) is int:
                    return slots_before(n) % 2
                return None

            def body(n, par):
                order = order_of(n)
                work_parity[0] = slots_before(n if type(n) is int else 2 - par) % 2
                work(order, n, par, slots_before(n), n + 1)

            work_parity = [0]
            inner = slot_parity

            def slot_parity(order, n):
                got = inner(order, n)
                return work_parity[0] if got is None else got

            work(prologue, 0, 0, 0, 0)
            iterations(pe, body)
            work(closing, NG, 0, slots_before(NG - 1) + 2, 0)

        @block.scalar
        def _(act):
            def copy_out(n):
                act.wait_ge(pv_done, n * NS)
                if not (type(n) is int and n == 1):
                    act.wait_ge(slot_full, last_slot(n - 1, order_of(n - 1), "ON"))
                for half in range(2):
                    nc.scalar.activation(o_sum[:, half * BANK:(half + 1) * BANK], bank(6 + half), ACT.Copy)\
                        .then_inc(o_ready, 1)

            def body(n, par):
                for s in range(NS):
                    w = len(steps[s]) * BANK
                    if not (type(n) is int and n == 0 and s < 2):
                        act.wait_ge(pv_done, n * NS + (s - 1))
                    for h in range(HG):
                        t = 4 * s + h
                        act.wait_ge(st_full, n * (4 * NS) + (t + 1))
                        nc.scalar.activation(prob[:, (par + s) % 2, h, 0:w],
                                             bank(2 + 2 * (t % 2), 2)[:, 0:w], ACT.Exp, scale=scale)\
                            .then_inc(exp_done, 1)
                    if s == 0 and not (type(n) is int and n == 0):
                        copy_out(n)
            iterations(act, body)
            copy_out(NG)

        @block.vector
        def _(dve):
            if decayed:
                dve.wait_ge(const_loaded, 32)
            else:
                nc.vector.memset(half_max[:, :, :, :], -3e38).then_inc(preset, 1)
                dve.wait_ge(preset, 1)

            def work(order, n, parity, base, chain, target):
                k = 0
                for kind, a, b in order:
                    if kind not in ("S", "MT", "ON"):
                        continue
                    at = bank((parity + k) % 2)
                    dve.wait_ge(slot_full, base + (k + 1))
                    if kind == "S" and units[a][2][5] is not None:
                        nc.vector.memset(spare[:, :], 0.0)
                    k += 1
                    if kind == "S":
                        h0, heads, i, half, width, diag = units[a][2]
                        if diag is not None:
                            nc.vector.tensor_tensor_reduce(
                                out=junk[:, :], in0=at, in1=diagonal[:, 3 * P - diag:3 * P - diag + BANK], scale=1.0,
                                scalar=-3e38, op0=ALU.mult, op1=ALU.max,
                                accum_out=half_max[:, h0, i, half:half + 1]).then_inc(slot_free, 1)
                        else:
                            nc.vector.tensor_reduce(
                                half_max[:, h0:h0 + heads, i, half],
                                at[:, 0:heads * width].rearrange("p (h w) -> p h w", w=width), AX.X, ALU.max)\
                                .then_inc(slot_free, 1)
                        if a == NU - 1:
                            dve.wait_ge(slot_free, base + k)
                            nc.vector.tensor_reduce(row_max[:, :, :], half_max[:, :, :, :], AX.X, ALU.max)\
                                .then_inc(max_ready, 1)
                    elif kind == "MT":
                        src = at[0:HG * KT, 0:P]
                        if not (type(target) is int and target == 0):
                            dve.wait_ge(m_loaded, target * (48 * len(variants)))
                        nc.vector.tensor_scalar(max_parts[:, 0, :], src, -1.0, None, ALU.mult)\
                            .then_inc(vector_done, 1)
                        chain = chain + 1
                        dve.wait_ge(vector_done, chain)
                        nc.vector.scalar_tensor_tensor(out=max_rest[:, :], in0=src, scalar=-1.0,
                                                       in1=max_parts[:, 0, :], op0=ALU.mult, op1=ALU.subtract)\
                            .then_inc(slot_free, 1)
                        dve.wait_ge(slot_free, base + k)
                        nc.vector.tensor_copy(max_parts[:, 1, :], max_rest[:, :]).then_inc(vector_done, 1)
                        chain = chain + 1
                        dve.wait_ge(vector_done, chain)
                        nc.vector.tensor_tensor(max_parts[:, 2, :], max_rest[:, :], max_parts[:, 1, :],
                                                ALU.subtract).then_inc(parts_ready, 1)
                    else:
                        view = at.rearrange("p (k h m) -> p k h m", k=4, h=HG)
                        nc.vector.reciprocal(inverse[:, a, :, :], view[:, :, :, D]).then_inc(vector_done, 1)
                        chain = chain + 1
                        dve.wait_ge(vector_done, chain)
                        dst = attn_tok[:, bass.ds(n - 1, 1), 4 * a:4 * a + 4, :, :]
                        nc.vector.tensor_tensor(
                            dst.rearrange("p o k h d -> p (o k) h d"), view[:, :, :, 0:D],
                            inverse[:, a, :, :].rearrange("p k (h o) -> p k h o", o=1).broadcast_to([P, 4, HG, D]),
                            ALU.mult).then_inc(slot_free, 1)

            def body(n, par):
                work(order_of(n), n, slots_before(n if type(n) is int else 2 - par) % 2, slots_before(n),
                     chain_before(n), n + 1)
            work(prologue, 0, 0, 0, 0, 0)
            iterations(dve, body)
            work(closing, NG, (slots_before(NG - 1) + 2) % 2, slots_before(NG - 1) + 2, chain_before(NG - 1) + 2, 0)


def output_phase(nc, sem, sb, ins, layer, attn_tok, x_tok, ident, bank):
    wo = sb("wo", [P, C], F32)
    bo = sb("bo", [P, C], F32)
    rows = sb("rows", [P, B, KT, HG, HG * D], F32)
    attnT = sb("attnT", [P, TOK], F32)
    with ExitStack() as c:
        loaded, packed, turned, attn_ready, out_ps, added = (
            c.enter_context(sem(s)) for s in ("loaded", "packed", "turned", "attn_ready", "out_ps", "added"))
        block = c.enter_context(nc.Block())

        @block.sync
        def _(sp):
            sp.dma_start(wo[:, :], ins["b_wo" if layer else "wo"]).then_inc(loaded, 16)
            if layer == 0:
                sp.dma_start(bo[:, :], ins["bo"].rearrange("(o n) -> o n", o=1).broadcast_to([P, C]))\
                    .then_inc(loaded, 16)

        @block.tensor
        def _(pe):
            for t in range(NT):
                b, k = divmod(t, KT)
                pe.wait_ge(packed, b + 1)
                src = rows[:, b, k, :, :].rearrange("p g m -> p (g m)")
                nc.tensor.transpose(bank(t // 4)[:, t % 4 * P:(t % 4 + 1) * P], src, ident[:, :]).then_inc(turned, 1)
            pe.wait_ge(loaded, 16 if layer else 32)
            for t in range(NT):
                pe.wait_ge(attn_ready, t // 4 + 1)
                nc.tensor.matmul(bank(4 + t // 4)[:, t % 4 * P:(t % 4 + 1) * P], attnT[:, t * P:(t + 1) * P],
                                 wo[:, :], start=True, stop=True).then_inc(out_ps, 1)

        @block.scalar
        def _(act):
            for k in range(CH):
                act.wait_ge(turned, 4 * (k + 1))
                nc.scalar.activation(attnT[:, k * BANK:(k + 1) * BANK], bank(k), ACT.Copy).then_inc(attn_ready, 1)

        @block.vector
        def _(dve):
            for b in range(B):
                nc.vector.tensor_copy(rows[:, b, :, :, :], attn_tok[:, b * HG:(b + 1) * HG, :, :, :]
                                      .rearrange("p g k h d -> p k g (h d)")).then_inc(packed, 1)
            flat = x_tok[:, :, :].rearrange("p t c -> p (t c)")
            dve.wait_ge(loaded, 16 if layer else 32)
            for k in range(CH):
                dve.wait_ge(out_ps, 4 * (k + 1))
                part = flat[:, k * BANK:(k + 1) * BANK]
                nc.vector.tensor_tensor(part, part, bank(4 + k), ALU.add).then_inc(added, 1)
            if layer == 0:
                dve.wait_ge(added, CH)
                nc.vector.tensor_tensor(x_tok[:, :, :], x_tok[:, :, :],
                                        bo[:, :].rearrange("p (o c) -> p o c", o=1).broadcast_to([P, NT, C]), ALU.add)


def route_phase(nc, sem, sb, ins, xnT, comb, ident, bank):
    SG, SE = 8 - TOPG, 8 - TOPK
    BIG = 1e30
    gate = sb("gate", [P, E], F32)
    bias = sb("bias", [P, E], F32)
    score = sb("score", [P, NT, E], F32)
    best = sb("best", [P, NT, GROUPS + SG], F32)
    best_left = sb("best_left", [P, NT, GROUPS + SG], F32)
    chosen = sb("chosen", [P, NT, GROUPS], F32)
    masked = sb("masked", [P, NT, E + SE], F32)
    left = sb("left", [P, NT, E + SE], F32)
    top = sb("top", [P, 2, NT, 8], F32)
    total = sb("total", [P, 2, NT], F32)
    parts = sb("parts", [E, 3, TOK], BF16)
    rest = sb("rest", [E, TOK], F32)
    with ExitStack() as c:
        loaded, logits, sigmoids, step, weights_ready, turned, first_ready, rest_ready, second_ready, third_ready, \
            moved, filled = (c.enter_context(sem(s)) for s in (
                "loaded", "logits", "sigmoids", "step", "weights_ready", "turned", "first_ready", "rest_ready",
                "second_ready", "third_ready", "moved", "filled"))
        block = c.enter_context(nc.Block())
        per = BANK // E

        @block.sync
        def _(sp):
            sp.dma_start(gate[:, :], ins["gate_w"]).then_inc(loaded, 16)
            sp.dma_start(bias[:, :], ins["gate_bias"].rearrange("(o n) -> o n", o=1).broadcast_to([P, E]))\
                .then_inc(loaded, 16)
            sp.wait_ge(third_ready, CH)
            for p in range(3):
                for half in range(2):
                    sp.dma_start(comb[32 * p:32 * p + 32, half, :], parts[32 * half:32 * half + 32, p, :])\
                        .then_inc(moved, 16)
            sp.wait_ge(moved, 6 * 16)

        @block.tensor
        def _(pe):
            pe.wait_ge(loaded, 32)
            for t in range(NT):
                nc.tensor.matmul(bank(t // per)[:, t % per * E:(t % per + 1) * E], xnT[:, t * P:(t + 1) * P],
                                 gate[:, :], start=True, stop=True).then_inc(logits, 1)
            pe.wait_ge(weights_ready, 1)
            for t in range(NT):
                nc.tensor.transpose(bank(4 + t // 4)[0:E, t % 4 * P:(t % 4 + 1) * P], score[:, t, :], ident[:, :])\
                    .then_inc(turned, 1)

        @block.gpsimd
        def _(pool):
            nc.gpsimd.memset(best[:, :, GROUPS:], BIG).then_inc(filled, 1)
            nc.gpsimd.memset(masked[:, :, E:], BIG).then_inc(filled, 1)
            for k in range(CH):
                chunk = slice(k * BANK, (k + 1) * BANK)
                pool.wait_ge(second_ready, k + 1)
                nc.gpsimd.tensor_tensor(parts[:, 2, chunk], rest[:, chunk], parts[:, 1, chunk], ALU.subtract)\
                    .then_inc(third_ready, 1)

        @block.scalar
        def _(act):
            for k in range(NT // per):
                act.wait_ge(logits, per * (k + 1))
                nc.scalar.activation(score[:, per * k:per * (k + 1), :].rearrange("p t e -> p (t e)"), bank(k),
                                     ACT.Sigmoid).then_inc(sigmoids, 1)
            for k in range(CH):
                chunk = slice(k * BANK, (k + 1) * BANK)
                act.wait_ge(turned, 4 * (k + 1))
                nc.scalar.activation(parts[:, 0, chunk], bank(4 + k)[0:E, :], ACT.Copy).then_inc(first_ready, 1)
            for k in range(CH):
                chunk = slice(k * BANK, (k + 1) * BANK)
                act.wait_ge(rest_ready, k + 1)
                nc.scalar.activation(parts[:, 1, chunk], rest[:, chunk], ACT.Copy).then_inc(second_ready, 1)

        @block.vector
        def _(dve):
            n = [0]

            def link(ins_):
                n[0] += 1
                ins_.then_inc(step, 1)
                dve.wait_ge(step, n[0])

            dve.wait_ge(loaded, 32)
            dve.wait_ge(sigmoids, NT // per)
            link(nc.vector.tensor_tensor(score[:, :, :], score[:, :, :],
                                         bias[:, :].rearrange("p (o e) -> p o e", o=1).broadcast_to([P, NT, E]),
                                         ALU.add))
            dve.wait_ge(filled, 2)
            link(nc.vector.tensor_reduce(best[:, :, 0:GROUPS],
                                         score[:, :, :].rearrange("p t (g e) -> p t g e", g=GROUPS), AX.X, ALU.max))
            for t in range(NT):
                last = nc.vector.max(top[:, 0, t, :], best[:, t, :])
            link(last)
            for t in range(NT):
                last = nc.vector.match_replace(best_left[:, t, :], top[:, 0, t, :], best[:, t, :], -BIG)
            link(last)
            link(nc.vector.tensor_tensor(chosen[:, :, :], best_left[:, :, 0:GROUPS], best[:, :, 0:GROUPS],
                                         ALU.not_equal))
            for g in range(GROUPS):
                e = E // GROUPS
                last = nc.vector.tensor_tensor(
                    masked[:, :, g * e:(g + 1) * e], score[:, :, g * e:(g + 1) * e],
                    chosen[:, :, g:g + 1].broadcast_to([P, NT, e]), ALU.mult)
            link(last)
            for t in range(NT):
                last = nc.vector.max(top[:, 1, t, :], masked[:, t, :])
            link(last)
            for t in range(NT):
                last = nc.vector.match_replace(left[:, t, :], top[:, 1, t, :], masked[:, t, :], -BIG)
            link(last)
            link(nc.vector.tensor_tensor(score[:, :, :], left[:, :, 0:E], masked[:, :, 0:E], ALU.not_equal))
            link(nc.vector.tensor_tensor(score[:, :, :], score[:, :, :], masked[:, :, 0:E], ALU.mult))
            link(nc.vector.tensor_reduce(total[:, 0, :], score[:, :, :], AX.X, ALU.add))
            link(nc.vector.tensor_scalar(total[:, 1, :], total[:, 0, :], 1e-8, None, ALU.add))
            link(nc.vector.reciprocal(total[:, 0, :], total[:, 1, :]))
            link(nc.vector.tensor_scalar(total[:, 1, :], total[:, 0, :], HS, None, ALU.mult))
            nc.vector.tensor_tensor(score[:, :, :], score[:, :, :],
                                    total[:, 1, :].rearrange("p (t o) -> p t o", o=1).broadcast_to([P, NT, E]),
                                    ALU.mult).then_inc(weights_ready, 1)
            for k in range(CH):
                chunk = slice(k * BANK, (k + 1) * BANK)
                dve.wait_ge(first_ready, k + 1)
                nc.vector.tensor_tensor(rest[:, chunk], bank(4 + k)[0:E, :], parts[:, 0, chunk], ALU.subtract)\
                    .then_inc(rest_ready, 1)


def expert_phase(nc, sem, sb, ins, xh, xl, comb, x_tok, ident, bank, out):
    NP = PAIRS + 1
    w32 = sb("w32", [P, 2, 3 * P], F32)
    wh = sb("wh", [P, 2, 3 * P], F16)
    wl = sb("wl", [P, 2, 3 * P], F16)
    pick = sb("pick", [96, 2, P], BF16)
    act_g = sb("act_g", [P, 2, BANK], F32)
    gated = sb("gated", [P, 2, BANK], F32)
    hidden = sb("hidden", [P, 2, BANK], F32)
    hh = sb("hh", [P, CH, BANK], F16)
    hl = sb("hl", [P, CH, BANK], F16)
    yT = sb("yT", [P, TOK], F32)
    LAG = 2
    SPLIT = 1
    UPPER, DOWN = slice(0, 2 * P), slice(2 * P, 3 * P)
    ACC, GATE, UP, WEIGHT = 0, 4, 5, 6
    with ExitStack() as c:
        pick_loaded, w_loaded = ([c.enter_context(sem(f"{s}_loaded{b}")) for b in range(2)] for s in ("pick", "w"))
        (upper_high, upper_low, down_high, down_low, gate_ps, up_ps, weight_ps, silu_done, gated_done,
         hidden_done, high_done, low_done, down_done, y_ready, turned, added, stored) = (
            c.enter_context(sem(s)) for s in (
                "upper_high", "upper_low", "down_high", "down_low", "gate_ps", "up_ps", "weight_ps",
                "silu_done", "gated_done", "hidden_done", "high_done", "low_done", "down_done", "y_ready", "turned",
                "added", "stored"))
        block = c.enter_context(nc.Block())

        def number(p, k):
            return p * CH + k

        @block.sync
        def _(sp):
            def load(p, par):
                sp.dma_start(w32[:, par, :], ins["experts"][bass.ds(p, 1)].rearrange("o p n -> (o p) n"))\
                    .then_inc(w_loaded[par], 16)

            def load_pick(p, par):
                sp.dma_start(pick[:, par, :], ins["pick"][bass.ds(p, 1)].rearrange("o r m -> (o r) m"))\
                    .then_inc(pick_loaded[par], 16)
            for p in range(2):
                load(p, p)
                load_pick(p, p)
            with sp.Fori(2, PAIRS, 2) as i:
                for par in range(2):
                    sp.wait_ge(down_low, i + (par - 1))
                    load(i + par, par)
                    sp.wait_ge(weight_ps, (i + (par - 1)) * CH)
                    load_pick(i + par, par)
            sp.wait_ge(down_low, PAIRS - 1)
            load(PAIRS, 0)
            if out is not None:
                o = out.rearrange("(t p) c -> p t c", p=P)
                for k in range(CH):
                    sp.wait_ge(added, k + 1)
                    sp.dma_start(o[:, 4 * k:4 * k + 4, :], x_tok[:, 4 * k:4 * k + 4, :]).then_inc(stored, 16)
                sp.wait_ge(stored, 16 * CH)

        @block.tensor
        def _(pe):
            def product(dst, par, m, high, low, first, last):
                w = slice(m * P, (m + 1) * P)
                nc.tensor.matmul(dst, wh[:, par, w], low, start=first, stop=False)
                nc.tensor.matmul(dst, wl[:, par, w], high, start=False, stop=False)
                return nc.tensor.matmul(dst, wh[:, par, w], high, start=False, stop=last)

            def pair(p, par, half):
                first = type(p) is int and p == 0
                shared = half is None
                pe.wait_ge(upper_low, p + 1)
                for k in range(CH):
                    chunk = slice(k * BANK, (k + 1) * BANK)
                    if not (first and k == 0):
                        pe.wait_ge(silu_done, number(p, k))
                    product(bank(GATE), par, 0, xh[:, chunk], xl[:, chunk], True, True).then_inc(gate_ps, 1)
                    if not (first and k == 0):
                        pe.wait_ge(hidden_done if shared and k else gated_done, number(p, k))
                    product(bank(UP), par, 1, xh[:, chunk], xl[:, chunk], True, True).then_inc(up_ps, 1)
                    if not shared:
                        if k == 0:
                            pe.wait_ge(pick_loaded[par], (p + (2 - par)) * 8)
                        if not (first and k == 0):
                            pe.wait_ge(hidden_done, number(p, k))
                        nc.tensor.matmul(bank(WEIGHT), pick[:, par, :], comb[:, half, chunk], start=True, stop=True)\
                            .then_inc(weight_ps, 1)
                    if not (first and k < LAG):
                        at = (k - LAG) % CH
                        of = par if k >= LAG else 1 - par
                        begins = type(p) is int and (p == 0 or (p == 1 and k < LAG))
                        if k == LAG:
                            pe.wait_ge(down_low, p + 1)
                        pe.wait_ge(low_done, number(p, k - LAG + 1))
                        product(bank(ACC + at), of, 2, hh[:, at, :], hl[:, at, :], begins,
                                shared and k >= LAG).then_inc(down_done, 1)

            pair(0, 0, 0)
            pair(1, 1, 0)
            for half in range(2):
                with pe.Fori(2 if half == 0 else PAIRS // 2, PAIRS // (2 - half), 2) as i:
                    pair(i, 0, half)
                    pair(i + 1, 1, half)
            pair(PAIRS, 0, None)
            for at in range(CH - LAG, CH):
                pe.wait_ge(low_done, number(PAIRS, at + 1))
                product(bank(ACC + at), 0, 2, hh[:, at, :], hl[:, at, :], False, True).then_inc(down_done, 1)
            for t in range(NT):
                pe.wait_ge(y_ready, t // 4 + 1)
                nc.tensor.transpose(bank(4 + t // 4)[:, t % 4 * P:(t % 4 + 1) * P], yT[:, t * P:(t + 1) * P],
                                    ident[:, :]).then_inc(turned, 1)

        @block.scalar
        def _(act):
            def high(p, k):
                act.wait_ge(hidden_done, number(p, k + 1))
                if not (type(p) is int and p == 0):
                    act.wait_ge(down_done, number(p, k + 1) - CH)
                nc.scalar.activation(hh[:, k, :], hidden[:, k % 2, :], ACT.Copy).then_inc(high_done, 1)

            def pair(p, shared=False):
                first = type(p) is int and p == 0
                for k in range(CH):
                    act.wait_ge(gate_ps, number(p, k + 1))
                    if not (first and k < 2):
                        act.wait_ge(hidden_done if shared and k >= 2 else gated_done, number(p, k - 1))
                    nc.scalar.activation(act_g[:, k % 2, :], bank(GATE), ACT.Silu, scale=1.0 / (XS * WS))\
                        .then_inc(silu_done, 1)
                    if k >= 1:
                        high(p, k - 1)
                    elif not first:
                        high(p - 1, CH - 1)
            pair(0)
            pair(1)
            with act.Fori(2, PAIRS, 2) as i:
                pair(i)
                pair(i + 1)
            pair(PAIRS, shared=True)
            high(PAIRS, CH - 1)
            for k in range(CH):
                act.wait_ge(down_done, number(PAIRS, k + 1))
                nc.scalar.activation(yT[:, k * BANK:(k + 1) * BANK], bank(ACC + k), ACT.Copy,
                                     scale=1.0 / (HS * WS)).then_inc(y_ready, 1)

        @block.vector
        def _(dve):
            def split(p, par, part, high, low):
                nc.vector.tensor_scalar(wh[:, par, part], w32[:, par, part], WS, None, ALU.mult).then_inc(high, 1)
                dve.wait_ge(high, p + 1)
                nc.vector.scalar_tensor_tensor(out=wl[:, par, part], in0=w32[:, par, part], scalar=WS,
                                               in1=wh[:, par, part], op0=ALU.mult, op1=ALU.subtract)\
                    .then_inc(low, 1)

            def split_upper(p, par, first=False):
                dve.wait_ge(w_loaded[par], (p + (2 - par)) * 8)
                if not first:
                    dve.wait_ge(up_ps, number(p - 1, 0))
                split(p, par, UPPER, upper_high, upper_low)

            def split_down(p, par, first=False):
                if not first:
                    dve.wait_ge(down_done, number(p - 1, 0))
                split(p, par, DOWN, down_high, down_low)

            def pair(p, par, shared=False):
                first = type(p) is int and p == 0
                for k in range(CH):
                    dve.wait_ge(up_ps, number(p, k + 1))
                    dve.wait_ge(silu_done, number(p, k + 1))
                    if not (first and k < 2):
                        dve.wait_ge(low_done, number(p, k - 1))
                    target = hidden if shared else gated
                    done = nc.vector.scalar_tensor_tensor(
                        out=target[:, k % 2, :], in0=bank(UP), scalar=(HS if shared else 1.0) / (XS * WS),
                        in1=act_g[:, k % 2, :], op0=ALU.mult, op1=ALU.mult)
                    if shared:
                        done.then_inc(hidden_done, 1)
                    else:
                        done.then_inc(gated_done, 1)
                        dve.wait_ge(gated_done, number(p, k + 1))
                        dve.wait_ge(weight_ps, number(p, k + 1))
                        nc.vector.tensor_tensor(hidden[:, k % 2, :], bank(WEIGHT), gated[:, k % 2, :], ALU.mult)\
                            .then_inc(hidden_done, 1)
                    if k == SPLIT and not shared:
                        split_upper(p + 1, 1 - par, first)
                    elif k == SPLIT + 1 and not shared:
                        split_down(p + 1, 1 - par, first)

            split_upper(0, 0, True)
            split_down(0, 0, True)
            pair(0, 0)
            pair(1, 1)
            with dve.Fori(2, PAIRS, 2) as i:
                pair(i, 0)
                pair(i + 1, 1)
            pair(PAIRS, 0, shared=True)
            flat = x_tok[:, :, :].rearrange("p t c -> p (t c)")
            for k in range(CH):
                dve.wait_ge(turned, 4 * (k + 1))
                part = flat[:, k * BANK:(k + 1) * BANK]
                nc.vector.tensor_tensor(part, part, bank(4 + k), ALU.add).then_inc(added, 1)

        @block.gpsimd
        def _(pool):
            def pair(p):
                for k in range(CH):
                    pool.wait_ge(high_done, number(p, k + 1))
                    nc.gpsimd.tensor_tensor(hl[:, k, :], hidden[:, k % 2, :], hh[:, k, :], ALU.subtract)\
                        .then_inc(low_done, 1)
            pair(0)
            pair(1)
            with pool.Fori(2, PAIRS, 2) as i:
                pair(i)
                pair(i + 1)
            pair(PAIRS)


def kernel(**inputs):
    import ml_dtypes
    import numpy as np
    import concourse.bacc as bacc
    from concourse.bass_utils import run_bass_kernel_spmd

    def get(n):
        return np.asarray(inputs[n])

    bf16 = ml_dtypes.bfloat16
    arrays = {"x": get("L0_attn_a_x").reshape(TOK, C)}
    for key, n in (("wq", "Wq"), ("bq", "bq"), ("wkd", "Wkd"), ("bkd", "bkd"), ("wku", "Wku"), ("bku", "bku"),
                   ("wo", "Wo"), ("bo", "bo")):
        arrays[key] = get("L0_attn_a_" + n)
    for key, n in (("b_wq", "W_q"), ("b_wk", "W_k"), ("b_wv", "W_v"), ("b_wo", "W_o"), ("b_wd", "W_down_kv"),
                   ("b_wuk", "W_up_k"), ("b_wuv", "W_up_v")):
        arrays[key] = get("L0_attn_b_" + n)
    arrays["gate_w"] = get("L0_ffn_gate_w").T
    arrays["gate_bias"] = get("L0_ffn_gate_bias")
    def up(w, s):
        return np.concatenate([get(w).reshape(PAIRS, P, C), get(s)[None]]).transpose(0, 2, 1)
    down = np.concatenate([get("L0_ffn_ed_w").transpose(0, 2, 1).reshape(PAIRS, P, C), get("L0_ffn_sd_w").T[None]])
    arrays["experts"] = np.concatenate([up("L0_ffn_eg_w", "L0_ffn_sg_w"), up("L0_ffn_eu_w", "L0_ffn_su_w"), down], 2)
    eye = np.eye(P, dtype=np.float32)
    arrays["ident"], arrays["ident_b"] = eye, eye.astype(bf16)
    at = np.arange(P)
    above = (at[None, :] > at[:, None]) * np.float32(-1e30)
    arrays["mask"] = np.stack([above, above.T, (at[:, None] <= at[None, :]) * np.float32(-1e30)]).astype(bf16)
    t = np.arange(T, dtype=np.float64)
    arrays["decay"] = np.exp(np.stack([-0.01 * t, 0.01 * t])).astype(np.float32)
    diagonal = np.ones((P, 7 * P), np.float32)
    diagonal[:, 3 * P:4 * P] = np.exp(-0.02 * np.maximum(0, at[None, :] - at[:, None]))
    arrays["diagonal"] = diagonal
    row, col, pair = np.arange(96)[None, :, None], np.arange(P)[None, None, :], np.arange(PAIRS + 1)[:, None, None]
    arrays["pick"] = (row % 32 == 2 * (pair % (PAIRS // 2)) + col // I).astype(bf16)

    nc = bacc.Bacc("TRN2", target_bir_lowering=False, num_devices=1)
    feed, ins = {}, {}
    for key, a in arrays.items():
        a = np.ascontiguousarray(a)
        feed[f"in_{key}"] = a
        ins[key] = nc.dram_tensor(f"in_{key}", a.shape, mybir.dt.from_np(a.dtype), kind="ExternalInput").ap()
    out = nc.dram_tensor("out_0", (TOK, C), F32, kind="ExternalOutput").ap()
    kernel_program(nc, ins, out)
    r = run_bass_kernel_spmd(nc, [feed], core_ids=[0])
    return r.results[0]["out_0"].reshape(B, T, C)
```

```python
from contextlib import ExitStack, nullcontext

import concourse.bass as bass
from concourse import mybir

F32 = mybir.dt.float32
BF16 = mybir.dt.bfloat16
F16 = mybir.dt.float16
ALU = mybir.AluOpType
ACT = mybir.ActivationFunctionType
AX = mybir.AxisListType
U32 = mybir.dt.uint32

P = 128
B, T, C, H = 2, 1024, 128, 16
D = C // H
TOK = B * T
NT = TOK // P
KT = T // P
HG = 4
NG = B * H // HG
BANK = 512
CH = TOK // BANK
TERMS = ((0, 0), (1, 0), (2, 0), (0, 1), (1, 1), (0, 2))
ROWS = len(TERMS) * D
MROW = 64
E, I, TOPK, GROUPS, TOPG = 64, 64, 6, 8, 4
PAIRS = E // 2
EPS = 1e-5
LAT = 32
XS, WS, HS = 16.0, 256.0, 16.0


HH = HG // 2


def score_units(decayed):
    units = []
    for i, first in [(i, first) for first in range(0, HG, HH) for i in range(KT)]:
        if decayed:
            for h in range(first, first + HH):
                for half in range(2):
                    k0, k1, mid = half * BANK, (half + 1) * BANK, (i + 1) * P
                    pieces = []
                    if k0 < mid:
                        pieces.append((h, i, k0, min(k1, mid), 0, 0))
                    if mid < k1:
                        pieces.append((h, i, max(k0, mid), k1, max(k0, mid) - k0, 1))
                    diagonal = i * P - k0 if i // 4 == half else None
                    units.append((pieces, [], (h, 1, i, half, BANK, diagonal)))
            continue
        for half in range(1 + i // 4):
            k0, k1 = half * BANK, min((i + 1) * P, (half + 1) * BANK)
            n = k1 - k0
            per = min(HH, BANK // n)
            for h0 in range(first, first + HH, per):
                pieces = [(h0 + a, i, k0, k1, a * n, 0) for a in range(per)]
                masked = [(a + 1) * n - P for a in range(per)] if k1 == (i + 1) * P else []
                units.append((pieces, masked, (h0, per, i, half, n, None)))
    return units


def key_banks(decayed):
    def seg(j, half, col):
        q0 = max(j * P, half * BANK)
        return (0, j, q0, (half + 1) * BANK, col, col if q0 == j * P else None)
    low = [[seg(0, 0, 0)], [seg(0, 1, 0)], [seg(1, 1, 0)], [seg(2, 1, 0)], [seg(3, 1, 0)], [seg(4, 1, 0)],
           [seg(1, 0, 0), seg(3, 0, 384)], [seg(2, 0, 0), seg(6, 1, 256)], [seg(5, 1, 0), seg(7, 1, 384)]]
    if not decayed:
        return low
    high = []
    for bank in low:
        segs = []
        for (_, j, q0, q1, col, diag) in bank:
            jj, a, b = KT - 1 - j, T - q1, T - q0
            segs.append((1, jj, a, b, col, None if diag is None else col + (b - a) - P))
        high.append(segs)
    return low + high


def kernel_program(nc, ins, out):
    ctx = ExitStack()
    uid = [0]

    def name(s):
        uid[0] += 1
        return f"{s}_{uid[0]}"

    sems, phase_number = {}, [0]

    def sem(s):
        key = (phase_number[0], s)
        if key not in sems:
            sems[key] = ctx.enter_context(nc.semaphore(f"{s}_{phase_number[0]}"))
        return nullcontext(sems[key])

    def next_phase():
        phase_number[0] += 1

    with ctx:
        def keep(s, shape, dt):
            return ctx.enter_context(nc.sbuf_tensor(s, shape, dt))

        ps = ctx.enter_context(nc.psum_tensor("ps", [P, 8 * BANK], F32))

        def bank(i, n=1):
            return ps[:, i * BANK:(i + n) * BANK]

        x_tok = keep("x_tok", [P, NT, C], F32)
        attn_tok = keep("attn_tok", [P, KT, NG, HG, D], F32)
        v_tok = keep("v_tok", [P, NG, KT, HG, D], F32)
        s_stack = [keep(f"s_{o}", [P, 2, HG, T], BF16) for o in "qk"]
        t_stack = [[keep(f"t_{o}_{b}", [P, 2, HG, T], BF16) for o in "qk"] for b in range(2)]
        scratch = [nc.dram_tensor(f"parts_{o}", [2, 3, NG, D, HG, T], BF16, kind="Internal").ap() for o in "qk"]
        col, row = (lambda a: a.rearrange("(p o) -> p o", o=1)), (lambda a: a.rearrange("(o n) -> o n", o=1))
        first = {"ident": (ins["ident"], [P, P], F32), "wq": (ins["wq"], [P, C], F32),
                 "bq": (col(ins["bq"]), [P, 1], F32), "wkd": (ins["wkd"], [P, 2 * LAT], F32),
                 "bkd": (col(ins["bkd"]), [2 * LAT, 1], F32),
                 "wk_low": (ins["wk_low"], [2 * LAT, C], F32), "bk": (col(ins["bk"]), [P, 1], F32),
                 "wv_low": (ins["wv_low"], [2 * LAT, C], F32),
                 "bv": (row(ins["bv"]).broadcast_to([P, C]), [P, C], F32)}
        later = {"ident_b": (ins["ident_b"], [P, P], BF16),
                 "mask": (ins["mask"].rearrange("m p n -> p m n"), [P, 3, P], BF16),
                 "wo": (ins["wo"], [P, C], F32), "bo": (row(ins["bo"]).broadcast_to([P, C]), [P, C], F32),
                 "gate": (ins["gate_w"], [P, E], F32),
                 "gate_bias": (row(ins["gate_bias"]).broadcast_to([P, E]), [P, E], F32),
                 "b_wq": (ins["b_wq"], [P, C], F32), "b_wk": (ins["b_wk"], [P, C], F32),
                 "b_wv": (ins["b_wv"], [P, C], F32), "b_wd": (ins["b_wd"], [P, LAT], F32),
                 "b_wuk": (ins["b_wuk"], [LAT, C], F32), "b_wuv": (ins["b_wuv"], [LAT, C], F32),
                 "b_wo": (ins["b_wo"], [P, C], F32), "diagonal": (ins["diagonal"], [P, 7 * P], F32)}
        w = {key: keep(f"w_{key}", shape, dt) for group in (first, later) for key, (_, shape, dt) in group.items()}
        ident = w["ident"]
        with sem("x_loaded") as x_loaded, sem("first_loaded") as first_loaded, sem("later_loaded") as later_loaded:
            loads = (x_loaded, (first_loaded, [(w[k], first[k][0]) for k in first]),
                     (later_loaded, [(w[k], later[k][0]) for k in later]))
        for layer in range(2):
            if layer == 1:
                clear_semaphores(nc, [s for (number, _), s in sems.items() if number >= 1])
            phase_number[0] = 1
            with ExitStack() as phase:
                def sb(s, shape, dt):
                    return phase.enter_context(nc.sbuf_tensor(name(s), shape, dt))
                xnT = sb("xnT", [P, TOK], F32)
                norm_phase(nc, sem, name, x_tok, w, xnT, None, None, bank,
                           (ins["x"], loads, s_stack, t_stack) if layer == 0 else None)
                next_phase()
                if layer == 0:
                    load_group = project_first(nc, sem, sb, w, xnT, v_tok, scratch, s_stack, t_stack, bank)
                else:
                    load_group = project_second(nc, sem, sb, ins, w, xnT, v_tok, scratch, s_stack, t_stack, bank)
            with ExitStack() as phase:
                def sb(s, shape, dt):
                    return phase.enter_context(nc.sbuf_tensor(name(s), shape, dt))
                next_phase()
                attention_phase(nc, sem, sb, layer == 1, w, x_tok, v_tok, load_group, s_stack, t_stack,
                                attn_tok, later_loaded, len(later), bank)
            with ExitStack() as phase:
                def sb(s, shape, dt):
                    return phase.enter_context(nc.sbuf_tensor(name(s), shape, dt))
                xh = sb("xh", [P, TOK], F16)
                xl = sb("xl", [P, TOK], F16)
                comb = sb("comb", [96, 2, TOK], BF16)
                parts = sb("weight_parts", [E, 3, TOK], BF16)
                w32 = sb("w32", [P, 2, 3 * P], F32)
                pick = sb("pick", [96, 2, P], BF16)
                with ExitStack() as route:
                    def rb(s, shape, dt):
                        return route.enter_context(nc.sbuf_tensor(name(s), shape, dt))
                    xnT = rb("xnT", [P, TOK], F32)
                    next_phase()
                    norm_phase(nc, sem, name, x_tok, w, xnT, (xh, xl), (attn_tok, w["b_wo" if layer else "wo"]), bank)
                    next_phase()
                    load_pair = route_phase(nc, sem, rb, ins, w, parts, comb, w32, pick, bank)
                next_phase()
                expert_phase(nc, sem, sb, ins, load_pair, xh, xl, comb, w32, pick, x_tok, ident, bank,
                             out if layer == 1 else None)


def clear_semaphores(nc, sems):
    numbers = sorted(s.num for s in sems)
    assert numbers == list(range(numbers[0], numbers[-1] + 1))
    with nc.Block() as block:
        @block.sync
        def _(sp):
            sp.sem_clear(range(numbers[0], numbers[-1] + 1))


def norm_phase(nc, sem, name, x_tok, w, xnT, halves, attention, bank, start=None):
    NC = NT // CH
    with ExitStack() as c:
        def sb(s, shape, dt):
            return c.enter_context(nc.sbuf_tensor(name(s), shape, dt))
        stats = sb("stats", [P, NT, 6], F32)
        mv = sb("mv", [P, NT, 2], F32)
        ve = sb("ve", [P, 4, NT], F32)
        xn = sb("xn", [P, NT, C], F32)
        if attention:
            attnT = sb("attnT", [P, TOK], F32)
        xnT_ready = c.enter_context(sem("xnT_ready"))
        (attn_turned, attn_ready, out_ps, added, stat_ready, var_ready, rstd_ready, shift_ready, xn_ready,
         turned, high_ready, zeroed) = (c.enter_context(sem(s)) for s in (
             "attn_turned", "attn_ready", "out_ps", "added", "stat_ready", "var_ready", "rstd_ready", "shift_ready",
             "xn_ready", "turned", "high_ready", "zeroed"))
        block = c.enter_context(nc.Block())
        ident = w["ident"]

        def tiles(k):
            return range(NC * k, NC * (k + 1))

        def columns(t):
            return slice(t % NC * P, (t % NC + 1) * P)

        if start:
            x, (x_loaded, (first_loaded, first), (later_loaded, later)), s_stack, t_stack = start

            @block.sync
            def _(sp):
                x_tiles = x.rearrange("(t p) c -> p t c", p=P)
                for k in range(CH):
                    sp.dma_start(x_tok[:, NC * k:NC * (k + 1), :], x_tiles[:, NC * k:NC * (k + 1), :])\
                        .then_inc(x_loaded, 16)
                for group, loaded in ((first, first_loaded), (later, later_loaded)):
                    for dst, src in group:
                        sp.dma_start(dst.ap(), src).then_inc(loaded, 16)

        @block.vector
        def _(dve):
            flat = x_tok[:, :, :].rearrange("p t c -> p (t c)")

            def statistics(k):
                if attention:
                    dve.wait_ge(out_ps, k + 1)
                    part = flat[:, k * BANK:(k + 1) * BANK]
                    nc.vector.tensor_tensor(part, part, bank(2 + k % 2), ALU.add).then_inc(added, 1)
                    dve.wait_ge(added, k + 1)
                elif start and k == 0:
                    dve.wait_ge(x_loaded, 16 * CH)
                for t in tiles(k):
                    nc.vector.bn_stats(stats[:, t, :], x_tok[:, t, :]).then_inc(stat_ready, 1)
                for t in tiles(k):
                    dve.wait_ge(stat_ready, NC * k + t + 1)
                    nc.vector.bn_aggr(mv[:, t, :], stats[:, t, :]).then_inc(stat_ready, 1)
                dve.wait_ge(stat_ready, 2 * NC * (k + 1))
                some = slice(NC * k, NC * (k + 1))
                nc.vector.tensor_scalar(ve[:, 0, some], mv[:, some, 1], EPS, None, ALU.add).then_inc(var_ready, 1)

            def normalise(k):
                some = slice(NC * k, NC * (k + 1))
                dve.wait_ge(rstd_ready, k + 1)
                nc.vector.scalar_tensor_tensor(out=ve[:, 3, some], in0=mv[:, some, 0], scalar=-1.0,
                                               in1=ve[:, 2, some], op0=ALU.mult, op1=ALU.mult)\
                    .then_inc(shift_ready, 1)
                dve.wait_ge(shift_ready, k + 1)
                for t in tiles(k):
                    nc.vector.tensor_scalar(xn[:, t, :], x_tok[:, t, :], ve[:, 2, t:t + 1], ve[:, 3, t:t + 1],
                                            ALU.mult, ALU.add).then_inc(xn_ready, 1)

            def low_half(k):
                if halves:
                    dve.wait_ge(high_ready, k + 1)
                    nc.vector.scalar_tensor_tensor(
                        out=halves[1][:, k * BANK:(k + 1) * BANK], in0=bank(4 + k), scalar=XS,
                        in1=halves[0][:, k * BANK:(k + 1) * BANK], op0=ALU.mult, op1=ALU.subtract)

            nc.vector.memset(ve[:, 1, :], -0.5)
            for k in range(CH + 2):
                if k < CH:
                    statistics(k)
                if 1 <= k <= CH:
                    normalise(k - 1)
                if k >= 2:
                    low_half(k - 2)

        @block.gpsimd
        def _(pool):
            if start:
                for stack in s_stack + t_stack[0]:
                    nc.gpsimd.memset(stack[:, 0].rearrange("p h t -> p (h t)").bitcast(U32), 0)
            for k in range(CH):
                some = slice(NC * k, NC * (k + 1))
                pool.wait_ge(var_ready, k + 1)
                nc.gpsimd.tensor_tensor(ve[:, 2, some], ve[:, 0, some], ve[:, 1, some], ALU.pow)\
                    .then_inc(rstd_ready, 1)

        @block.tensor
        def _(pe):
            if attention:
                attn_tok, wo = attention

                def turn(k):
                    for t in tiles(k):
                        b, i = divmod(t, KT)
                        src = attn_tok[:, i, b * HG:(b + 1) * HG, :, :].rearrange("p g h d -> p (g h d)")
                        last = nc.tensor.transpose(bank(k % 2)[:, columns(t)], src, ident[:, :])
                    last.then_inc(attn_turned, 1)
                turn(0)
                turn(1)
                for k in range(CH):
                    pe.wait_ge(attn_ready, k + 1)
                    if k >= 2:
                        pe.wait_ge(added, k - 1)
                    for t in tiles(k):
                        last = nc.tensor.matmul(bank(2 + k % 2)[:, columns(t)], attnT[:, t * P:(t + 1) * P], wo[:, :],
                                                start=True, stop=True)
                    last.then_inc(out_ps, 1)
                    if k + 2 < CH:
                        turn(k + 2)
            elif start:
                pe.wait_ge(first_loaded, 16 * len(first))

            def logits(k):
                pe.wait_ge(xnT_ready, k + 1)
                for t in tiles(k):
                    nc.tensor.matmul(bank(k // 2)[:, t % 8 * E:(t % 8 + 1) * E], xnT[:, t * P:(t + 1) * P],
                                     w["gate"][:, :], start=True, stop=True)
            for t in range(NT):
                pe.wait_ge(xn_ready, t + 1)
                nc.tensor.transpose(bank(4 + t // NC)[:, columns(t)], xn[:, t, :], ident[:, :]).then_inc(turned, 1)
                if halves and t % NC == NC - 1 and t >= NC:
                    logits(t // NC - 1)
            if halves:
                logits(CH - 1)

        @block.scalar
        def _(act):
            if attention:
                for k in range(CH):
                    act.wait_ge(attn_turned, k + 1)
                    nc.scalar.activation(attnT[:, k * BANK:(k + 1) * BANK], bank(k % 2), ACT.Copy)\
                        .then_inc(attn_ready, 1)
            for k in range(CH):
                act.wait_ge(turned, NC * (k + 1))
                chunk = slice(k * BANK, (k + 1) * BANK)
                nc.scalar.activation(xnT[:, chunk], bank(4 + k), ACT.Copy).then_inc(xnT_ready, 1)
                if halves:
                    act.wait_ge(xnT_ready, k + 1)
                    nc.scalar.activation(halves[0][:, chunk], bank(4 + k), ACT.Copy, scale=XS).then_inc(high_ready, 1)


class SplitJobs:

    def __init__(self, nc, sem, sb, c, jobs, scratch):
        self.nc, self.jobs, self.scratch = nc, jobs, scratch
        self.value = sb("value", [P, self.VALUES, BANK], F32)
        self.rest = sb("rest", [P, self.RESTS, BANK], F32)
        self.parts = sb("parts", [P, self.PARTS, 3, BANK], BF16)
        self.value_ready, self.first_ready, self.rest_ready, self.second_ready, self.third_ready = (
            c.enter_context(sem(s)) for s in ("value_ready", "first_ready", "rest_ready", "second_ready",
                                              "third_ready"))
        self.stored = [c.enter_context(sem(f"stored{i}")) for i in range(self.PARTS)]

    VALUES, RESTS, PARTS = 4, 3, 6

    def vector(self, dve, make_value, make_v):
        nc, n = self.nc, len(self.jobs)
        for j in range(n + 2):
            if j == n // 2 + 2:
                make_v(0)
            if j < n:
                if j >= self.VALUES:
                    dve.wait_ge(self.rest_ready, j - self.VALUES + 1)
                make_value(j, self.value[:, j % self.VALUES, :]).then_inc(self.value_ready, 1)
            i = j - 2
            if i >= 0:
                dve.wait_ge(self.first_ready, i + 1)
                if i >= self.RESTS:
                    dve.wait_ge(self.third_ready, i - self.RESTS + 1)
                nc.vector.tensor_tensor(self.rest[:, i % self.RESTS, :], self.value[:, i % self.VALUES, :],
                                        self.parts[:, i % self.PARTS, 0, :], ALU.subtract).then_inc(self.rest_ready, 1)
        make_v(1)

    def scalar(self, act, at=None, then=None):
        nc, n = self.nc, len(self.jobs)
        for j in range(n + 2):
            if j == at:
                then()
            if j < n:
                act.wait_ge(self.value_ready, j + 1)
                if j >= self.PARTS:
                    act.wait_ge(self.stored[j % self.PARTS], 16 * (j // self.PARTS))
                nc.scalar.activation(self.parts[:, j % self.PARTS, 0, :], self.value[:, j % self.VALUES, :], ACT.Copy)\
                    .then_inc(self.first_ready, 1)
            i = j - 2
            if i >= 0:
                act.wait_ge(self.rest_ready, i + 1)
                nc.scalar.activation(self.parts[:, i % self.PARTS, 1, :], self.rest[:, i % self.RESTS, :], ACT.Copy)\
                    .then_inc(self.second_ready, 1)

    def gpsimd(self, pool):
        for j in range(len(self.jobs)):
            pool.wait_ge(self.second_ready, j + 1)
            self.nc.gpsimd.tensor_tensor(self.parts[:, j % self.PARTS, 2, :], self.rest[:, j % self.RESTS, :],
                                         self.parts[:, j % self.PARTS, 1, :], ALU.subtract).then_inc(self.third_ready, 1)

    def sync(self, sp, loader):
        load_half = loader[1]
        half = len(self.jobs) // 2

        def store(j):
            operand, variant, k = self.jobs[j]
            sp.wait_ge(self.third_ready, j + 1)
            b, t0 = k * BANK // T, k * BANK % T
            dst = self.scratch[operand][variant, :, b * HG:(b + 1) * HG, :, :, t0:t0 + BANK]
            sp.dma_start(dst.rearrange("m g d h t -> (g d h) m t"), self.parts[:, j % self.PARTS, :, :])\
                .then_inc(self.stored[j % self.PARTS], 16)

        def all_stored(n):
            for i in range(self.PARTS):
                sp.wait_ge(self.stored[i], 16 * len([j for j in range(n) if j % self.PARTS == i]))
        for j in range(half):
            store(j)
        all_stored(half)
        for j in range(half, len(self.jobs)):
            store(j)
            if j < half + 2:
                load_half(sp, 0, 0, (j - half,))
        all_stored(len(self.jobs))


def group_loader(sem, c, scratch, s_stack, t_stack, variants):
    s_loaded = [c.enter_context(sem(f"s_loaded{b}")) for b in range(2)]
    t_loaded = [c.enter_context(sem(f"t_loaded{b}")) for b in range(2)]

    def load(sp, stack, n, loaded, h0=0, h1=HG, sides=(0, 1)):
        for side in sides:
            for v in variants:
                row = 0
                for terms in (3, 2, 1):
                    rows = stack[side][row:row + terms * D, v, h0:h1].rearrange("r h t -> r (h t)")
                    if side == 0:
                        src = scratch[0][v, 0:terms, bass.ds(n, 1), :, h0:h1].rearrange("m o d h t -> m (o d) (h t)")
                    else:
                        src = scratch[1][v, 3 - terms:4 - terms, bass.ds(n, 1), :, h0:h1]\
                            .rearrange("m o d h t -> m (o d) (h t)").broadcast_to([terms, D, (h1 - h0) * T])
                    sp.dma_start(rows, src).then_inc(loaded, 16)
                    row += terms * D

    def load_half(sp, n, half, sides=(0, 1)):
        load(sp, s_stack, n, s_loaded[half], half * HH, (half + 1) * HH, sides)
    return load, load_half, s_loaded, t_loaded, 6 * 16 * len(variants)


PRODUCTS = [(o, k) for b in range(B) for o in range(2) for k in range(b * CH // B, (b + 1) * CH // B)]


def v_chunk(nc, pe, k, latent, wv, v_ps, v_taken, bank):
    if k >= 2:
        pe.wait_ge(v_taken, k - 1)
    for t in range(4 * k, 4 * k + 4):
        last = nc.tensor.matmul(bank(6 + k % 2)[:, t % 4 * P:(t % 4 + 1) * P], latent[:, t * P:(t + 1) * P],
                                wv[:, :], start=True, stop=True)
    last.then_inc(v_ps, 1)


def v_places(v_tok, k, bank):
    b, j = divmod(4 * k, KT)
    dst = v_tok[:, b * HG:(b + 1) * HG, j:j + 4, :, :].rearrange("p g k h d -> p g k (h d)")
    return dst, bank(6 + k % 2).rearrange("p (k g m) -> p g k m", k=4, g=HG)


def project_first(nc, sem, sb, w, xnT, v_tok, scratch, s_stack, t_stack, bank):
    latent = sb("latent", [2 * LAT, TOK], F32)
    with ExitStack() as c:
        latent_ps, latent_ready, qk_ps, v_ps, v_taken, zeroed = (
            c.enter_context(sem(s)) for s in ("latent_ps", "latent_ready", "qk_ps", "v_ps", "v_taken", "zeroed"))
        loader = group_loader(sem, c, scratch, s_stack, t_stack, range(1))
        jobs = [(o, 0, k) for o, k in PRODUCTS]
        split = SplitJobs(nc, sem, sb, c, jobs, scratch)
        block = c.enter_context(nc.Block())

        @block.sync
        def _(sp):
            sp.wait_ge(zeroed, 4)
            split.sync(sp, loader)

        @block.tensor
        def _(pe):
            for j, (o, k) in enumerate(PRODUCTS):
                chunk = slice(k * BANK, (k + 1) * BANK)
                if j == 2:
                    for i in range(CH):
                        nc.tensor.matmul(bank(i)[0:2 * LAT, :], w["wkd"][:, :], xnT[:, i * BANK:(i + 1) * BANK],
                                         start=True, stop=True).then_inc(latent_ps, 1)
                if j >= 2:
                    pe.wait_ge(split.value_ready, j - 1)
                if o == 1:
                    pe.wait_ge(latent_ready, k + 1)
                weights, values = ((w["wq"], xnT), (w["wk_low"], latent))[o]
                nc.tensor.matmul(bank(4 + j % 2), weights[:, :], values[:, chunk], start=True, stop=True)\
                    .then_inc(qk_ps, 1)
                if j in (3, 7):
                    for i in range(j // 2 - 1, j // 2 + 1):
                        v_chunk(nc, pe, i, latent, w["wv_low"], v_ps, v_taken, bank)

        @block.scalar
        def _(act):
            for k in range(CH):
                act.wait_ge(latent_ps, k + 1)
                nc.scalar.activation(latent[:, k * BANK:(k + 1) * BANK], bank(k)[0:2 * LAT, :], ACT.Gelu,
                                     bias=w["bkd"][:, 0:1]).then_inc(latent_ready, 1)
            split.scalar(act)

        @block.gpsimd
        def _(pool):
            for stack in t_stack[1]:
                nc.gpsimd.memset(stack[:, 0].rearrange("p h t -> p (h t)").bitcast(U32), 0).then_inc(zeroed, 1)
            for b in range(2):
                pool.wait_ge(zeroed, 2 + b)
                pool_ones(nc, t_stack[b][1], 0).then_inc(zeroed, 1)
            pool.wait_ge(zeroed, 4)
            split.gpsimd(pool)

        @block.vector
        def _(dve):
            def value(j, dst):
                dve.wait_ge(qk_ps, j + 1)
                bias = w[("bq", "bk")[jobs[j][0]]]
                return nc.vector.tensor_scalar(dst, bank(4 + j % 2), bias[:, 0:1], None, ALU.add)
            bv = w["bv"][:, :].rearrange("p (g k m) -> p g k m", g=HG, k=1).broadcast_to([P, HG, 4, HG * D])

            def make_v(b):
                for k in range(b * CH // B, (b + 1) * CH // B):
                    dve.wait_ge(v_ps, k + 1)
                    dst, src = v_places(v_tok, k, bank)
                    nc.vector.tensor_tensor(dst, src, bv, ALU.add).then_inc(v_taken, 1)
            split.vector(dve, value, make_v)
    return loader


def pool_ones(nc, stack, v):
    return nc.gpsimd.memset(stack[MROW:MROW + 3, v].rearrange("p h t -> p (h t)").bitcast(U32), 0x3F803F80)


def project_second(nc, sem, sb, ins, w, xnT, v_tok, scratch, s_stack, t_stack, bank):
    decay = sb("decay", [P, 2, T], F32)
    kv = sb("kv", [P, TOK], F32)
    latent = sb("latent", [LAT, TOK], F32)
    with ExitStack() as c:
        decay_loaded, kv_ps, kv_ready, latent_ps, latent_ready, qk_ps, v_ps, v_taken, zeroed = (
            c.enter_context(sem(s)) for s in ("decay_loaded", "kv_ps", "kv_ready", "latent_ps", "latent_ready",
                                              "qk_ps", "v_ps", "v_taken", "zeroed"))
        loader = group_loader(sem, c, scratch, s_stack, t_stack, range(2))
        jobs = [(o, v, k) for o, k in PRODUCTS for v in range(2)]
        split = SplitJobs(nc, sem, sb, c, jobs, scratch)
        block = c.enter_context(nc.Block())

        @block.sync
        def _(sp):
            for v in range(2):
                sp.dma_start(decay[:, v, :], ins["decay"][v:v + 1, :].broadcast_to([P, T])).then_inc(decay_loaded, 16)
            split.sync(sp, loader)

        @block.tensor
        def _(pe):
            def latents(b):
                for k in range(b * CH // B, (b + 1) * CH // B):
                    chunk = slice(k * BANK, (k + 1) * BANK)
                    nc.tensor.matmul(bank(k), w["b_wk"][:, :], xnT[:, chunk], start=True, stop=False)
                    nc.tensor.matmul(bank(k), w["b_wv"][:, :], xnT[:, chunk], start=False, stop=True)\
                        .then_inc(kv_ps, 1)
                for k in range(b * CH // B, (b + 1) * CH // B):
                    pe.wait_ge(kv_ready, k + 1)
                    nc.tensor.matmul(bank(k)[0:LAT, :], w["b_wd"][:, :], kv[:, k * BANK:(k + 1) * BANK],
                                     start=True, stop=True).then_inc(latent_ps, 1)

            for m, (o, k) in enumerate(PRODUCTS):
                chunk = slice(k * BANK, (k + 1) * BANK)
                if m in (2, 4):
                    latents(m // 2 - 1)
                if m >= 2:
                    pe.wait_ge(split.value_ready, 2 * (m - 1))
                if o == 1:
                    pe.wait_ge(latent_ready, k + 1)
                weights, values = ((w["b_wq"], xnT), (w["b_wuk"], latent))[o]
                nc.tensor.matmul(bank(4 + m % 2), weights[:, :], values[:, chunk], start=True, stop=True)\
                    .then_inc(qk_ps, 1)
                if m in (3, 7):
                    for i in range(m // 2 - 1, m // 2 + 1):
                        v_chunk(nc, pe, i, latent, w["b_wuv"], v_ps, v_taken, bank)

        @block.scalar
        def _(act):
            def latents(b):
                for k in range(b * CH // B, (b + 1) * CH // B):
                    act.wait_ge(kv_ps, k + 1)
                    nc.scalar.activation(kv[:, k * BANK:(k + 1) * BANK], bank(k), ACT.Copy).then_inc(kv_ready, 1)
                for k in range(b * CH // B, (b + 1) * CH // B):
                    act.wait_ge(latent_ps, k + 1)
                    nc.scalar.activation(latent[:, k * BANK:(k + 1) * BANK], bank(k)[0:LAT, :], ACT.Copy)\
                        .then_inc(latent_ready, 1)
            latents(0)
            split.scalar(act, at=4, then=lambda: latents(1))

        @block.gpsimd
        def _(pool):
            nc.gpsimd.memset(t_stack[1][0][MROW:MROW + 3, 0].rearrange("p h t -> p (h t)").bitcast(U32), 0)\
                .then_inc(zeroed, 1)
            pool.wait_ge(zeroed, 1)
            split.gpsimd(pool)

        @block.vector
        def _(dve):
            dve.wait_ge(decay_loaded, 32)

            def value(j, dst):
                o, v, k = jobs[j]
                dve.wait_ge(qk_ps, j // 2 + 1)
                t0 = k * BANK % T
                factor = decay[:, v if o == 0 else 1 - v, t0:t0 + BANK]
                return nc.vector.tensor_tensor(dst, bank(4 + j // 2 % 2), factor, ALU.mult)

            def make_v(b):
                for k in range(b * CH // B, (b + 1) * CH // B):
                    dve.wait_ge(v_ps, k + 1)
                    dst, src = v_places(v_tok, k, bank)
                    nc.vector.tensor_copy(dst, src).then_inc(v_taken, 1)
            split.vector(dve, value, make_v)
    return loader


def attention_phase(nc, sem, sb, decayed, w, x_tok, v_tok, loader, s_stack, t_stack, attn_tok, later_loaded,
                    n_later, bank):
    stack_load, load_half, s_loaded, t_loaded, LOADED = loader
    ident, ident_b, mask, diagonal = w["ident"], w["ident_b"], w["mask"], w["diagonal"]
    variants = range(2 if decayed else 1)
    units, banks = score_units(decayed), key_banks(decayed)
    steps = [banks[i:i + 2] for i in range(0, len(banks), 2)]
    NU, NS = len(units), len(steps)
    scale = (C if decayed else D) ** -0.5
    NV = len(variants)

    prob = sb("prob", [P, 2, HG, 2 * BANK], F32)
    v_group = sb("v_group", [P, 2, KT, HG, 32], F32)
    o_sum = sb("o_sum", [P, T], F32)
    half_max = sb("half_max", [P, HG, KT, 2], F32)
    row_max = sb("row_max", [P, 3, HG * KT], F32)
    MR = HG * KT
    max_parts = sb("max_parts", [3 * MR, P], BF16)
    max_second = sb("max_second", [3 * MR, P], BF16)
    max_rest = sb("max_rest", [3 * MR, P], F32)
    inverse = sb("inverse", [P, 2, 4, HG], F32)
    if decayed:
        junk = sb("junk", [P, 2, BANK], BF16)
        spare = sb("spare", [P, 2], F32)

    def schedule(with_scores, with_norm):
        main = []
        for s in range(NS):
            products = [("PV", s - 1, b) for b in range(len(steps[s - 1]))] if s > 0 else \
                [("END", NS - 1, b) for b in range(len(steps[-1]))] if with_norm else []
            main += [("ST", s, 0), ("ST", s, 1)] + products[:1] + [("ST", s, 2)] + products[1:] + [("ST", s, 3)]
            if s == 1 and with_norm:
                main += [("ON", 0, 0), ("ON", 1, 0)]
        if not with_scores:
            return main
        cost = {"ST": 4, "PV": 8, "END": 8, "ON": 4}
        whole = sum(cost[kind] for kind, _, _ in main)
        done, passed, turn = (0 if with_norm else AHEAD), 0, None
        order = [("S", u, 0) for u in range(done)]
        for item in main:
            order.append(item)
            passed += cost[item[0]]
            if turn is not None and passed >= turn:
                order.append(("MT", 0, 0))
                turn = None
            upto = max(done, min(NU, int(NU * passed / (SPREAD * whole))))
            order += [("S", u, 0) for u in range(done, upto)]
            if done < NU <= upto:
                turn = passed + 8
            done = upto
        assert turn is None
        return order

    def slots_before(n):
        return NU + 1 if type(n) is int and n == 0 else (n - 1) * (NU + 3) + 2 * (NU + 1)

    def chain_before(n):
        return 3 if type(n) is int and n == 0 else (n - 1) * 5 + 6

    def last_slot(n, order, kind, count=None):
        kinds = [k for k, _, _ in order if k in ("S", "MT", "ON")]
        return slots_before(n) + ([i for i, k in enumerate(kinds) if k == kind][:count][-1] + 1)

    SPREAD, AHEAD = 0.85, 10
    prologue = [("S", u, 0) for u in range(NU)] + [("MT", 0, 0)]
    first, middle, final = schedule(True, False), schedule(True, True), schedule(False, True)
    closing = [("END", NS - 1, b) for b in range(len(steps[-1]))] + [("ON", 0, 0), ("ON", 1, 0)]

    def order_of(n):
        return first if type(n) is int and n == 0 else final if type(n) is int and n == NG - 1 else middle

    def iterations(eng, body):
        body(0, 0)
        with eng.Fori(1, NG - 1, 2) as i:
            body(i, 1)
            body(i + 1, 0)
        body(NG - 1, 1)

    with ExitStack() as c:
        (v_preset, v_ready, m_loaded, slot_full, slot_free, st_full, exp_done, pv_done,
         o_ready, max_ready, parts_ready, vector_done, preset, zeroed) = (
            c.enter_context(sem(s)) for s in (
                "v_preset", "v_ready", "m_loaded", "slot_full", "slot_free", "st_full",
                "exp_done", "pv_done", "o_ready", "max_ready", "parts_ready", "vector_done", "preset", "zeroed"))
        block = c.enter_context(nc.Block())

        @block.sync
        def _(sp):
            def maxima_load(par):
                for v in variants:
                    sp.dma_start(t_stack[par][0][MROW:MROW + 3, v, :, :], max_parts[:, :]).then_inc(m_loaded, 16)

            def body(n, par, with_scores=True):
                sp.wait_ge(st_full, n * (4 * NS))
                stack_load(sp, t_stack[1 - par], n + 1, t_loaded[1 - par])
                if with_scores:
                    sp.wait_ge(slot_full, last_slot(n, order_of(n), "S", NU // 2))
                    load_half(sp, n + 2, 0)
                sp.wait_ge(parts_ready, n + 2)
                maxima_load(1 - par)
                if with_scores:
                    load_half(sp, n + 2, 1)

            load_half(sp, 0, 1)
            for n in range(2):
                stack_load(sp, t_stack[n], n, t_loaded[n])
            sp.wait_ge(parts_ready, 1)
            maxima_load(0)
            for half in range(2):
                load_half(sp, 2, half)
            sp.wait_ge(parts_ready, 2)
            maxima_load(1)
            with sp.Fori(1, NG - 3, 2) as i:
                body(i, 1)
                body(i + 1, 0)
            body(NG - 3, 1)
            body(NG - 2, 0, with_scores=False)

        @block.tensor
        def _(pe):
            pe.wait_ge(later_loaded, 16 * n_later)

            def work(order, n, par, slot, target):
                base = slot
                parity = slot_parity(order, n)
                k = 0
                for kind, a, b in order:
                    if kind in ("S", "MT", "ON"):
                        at = bank((parity + k) % 2)
                        if not (type(base) is int and base + k < 2):
                            pe.wait_ge(slot_free, base + (k - 1))
                        k += 1
                    if kind == "S":
                        second = type(target) is int and target == 1
                        stack = t_stack[1] if second else s_stack
                        if a == 0 and second:
                            pe.wait_ge(t_loaded[1], LOADED)
                        elif a in (0, NU // 2) and not second:
                            pe.wait_ge(s_loaded[a // (NU // 2)],
                                       LOADED if type(target) is int and target == 0 else target * LOADED)
                        pieces, masked, _ = units[a]
                        todo = []
                        for (h, i, k0, k1, col, v) in pieces:
                            todo.append((at[:, col:col + k1 - k0], stack[0][:, v, h, i * P:(i + 1) * P],
                                         stack[1][:, v, h, k0:k1], True, (k1 - k0 + col - P) not in masked))
                            if k1 - k0 + col - P in masked:
                                col = k1 - k0 + col - P
                                todo.append((at[:, col:col + P], ident_b[:, :], mask[:, 0, :], False, True))
                        for o, l, r, st, sp_ in todo:
                            last = nc.tensor.matmul(o, l, r, start=st, stop=sp_)
                        last.then_inc(slot_full, 1)
                    elif kind == "MT":
                        pe.wait_ge(max_ready, target + 1)
                        nc.tensor.transpose(at[0:3 * MR, 0:P], row_max[:, :, :].rearrange("p m r -> p (m r)"),
                                            ident[:, :]).then_inc(slot_full, 1)
                    elif kind == "ON":
                        if a == 0:
                            pe.wait_ge(o_ready, n * 2)
                        for q in range(4):
                            last = nc.tensor.transpose(at[:, q * P:(q + 1) * P],
                                                       o_sum[:, (4 * a + q) * P:(4 * a + q + 1) * P], ident[:, :])
                        last.then_inc(slot_full, 1)
                    elif kind == "ST":
                        if a == 0 and b == 0:
                            pe.wait_ge(t_loaded[par], (n + (2 - par)) * (LOADED // 2))
                            pe.wait_ge(m_loaded, (n + 1) * (16 * NV))
                        t = 4 * a + b
                        if not (type(n) is int and n == 0 and t < 2):
                            pe.wait_ge(exp_done, n * (4 * NS) + (t - 1))
                        for x, segs in enumerate(steps[a]):
                            for (v, j, q0, q1, col, diag) in segs:
                                dst = bank(2 + 2 * (t % 2) + x)
                                last = nc.tensor.matmul(dst[:, col:col + q1 - q0],
                                                        t_stack[par][1][:, v, b, j * P:(j + 1) * P],
                                                        t_stack[par][0][:, v, b, q0:q1],
                                                        start=True, stop=diag is None)
                                if diag is not None:
                                    last = nc.tensor.matmul(dst[:, diag:diag + P], ident_b[:, :], mask[:, 1 + v, :],
                                                            start=False, stop=True)
                        last.then_inc(st_full, 1)
                    elif kind == "PV":
                        if a == 0 and b == 0:
                            pe.wait_ge(v_ready, n + 1)
                            if not (type(n) is int and n == 0):
                                pe.wait_ge(o_ready, n * 2)
                        if b == 0:
                            pe.wait_ge(exp_done, n * (4 * NS) + 4 * (a + 1))
                        product(a, b, par)
                    elif kind == "END":
                        if b == 0:
                            pe.wait_ge(exp_done, n * (4 * NS))
                        product(a, b, 1 - par)

            def product(a, b, par):
                for (v, j, q0, q1, col, _) in steps[a][b]:
                    half = q0 // BANK
                    ends = last_of_half[half] == (a, b, j)
                    for h in range(HG):
                        last = nc.tensor.matmul(
                            bank(6 + half)[32 * h:32 * h + 32, q0 - half * BANK:q1 - half * BANK],
                            v_group[:, par, j, h, :],
                            prob[:, (par + a) % 2, h, b * BANK + col:b * BANK + col + q1 - q0],
                            start=(a == 0), stop=ends, skip_group_check=True)
                if b == len(steps[a]) - 1:
                    last.then_inc(pv_done, 1)

            last_of_half = {}
            for a, st in enumerate(steps):
                for b, segs in enumerate(st):
                    for seg in segs:
                        last_of_half[seg[2] // BANK] = (a, b, seg[1])

            def slot_parity(order, n):
                if order is prologue:
                    return 0
                if order is closing:
                    return (slots_before(NG - 1) + 2) % 2
                if type(n) is int:
                    return slots_before(n) % 2
                return None

            def body(n, par):
                order = order_of(n)
                work_parity[0] = slots_before(n if type(n) is int else 2 - par) % 2
                work(order, n, par, slots_before(n), n + 1)

            work_parity = [0]
            inner = slot_parity

            def slot_parity(order, n):
                got = inner(order, n)
                return work_parity[0] if got is None else got

            work(prologue, 0, 0, 0, 0)
            iterations(pe, body)
            work(closing, NG, 0, slots_before(NG - 1) + 2, 0)

        @block.scalar
        def _(act):
            def copy_out(n):
                act.wait_ge(pv_done, n * NS)
                if not (type(n) is int and n == 1):
                    act.wait_ge(slot_full, last_slot(n - 1, order_of(n - 1), "ON"))
                for half in range(2):
                    nc.scalar.activation(o_sum[:, half * BANK:(half + 1) * BANK], bank(6 + half), ACT.Copy)\
                        .then_inc(o_ready, 1)

            def body(n, par):
                for s in range(NS):
                    w = len(steps[s]) * BANK
                    if not (type(n) is int and n == 0 and s < 2):
                        act.wait_ge(pv_done, n * NS + (s - 1))
                    for h in range(HG):
                        t = 4 * s + h
                        act.wait_ge(st_full, n * (4 * NS) + (t + 1))
                        nc.scalar.activation(prob[:, (par + s) % 2, h, 0:w],
                                             bank(2 + 2 * (t % 2), 2)[:, 0:w], ACT.Exp, scale=scale)\
                            .then_inc(exp_done, 1)
                    if s == 0 and not (type(n) is int and n == 0):
                        copy_out(n)
            iterations(act, body)
            copy_out(NG)

        @block.gpsimd
        def _(pool):
            def values(n, par):
                nc.gpsimd.tensor_copy(v_group[:, par, :, :, 0:D],
                                      v_tok[:, bass.ds(n, 1)].rearrange("p o k h d -> p (o k) h d"))\
                    .then_inc(v_ready, 1)

            nc.gpsimd.memset(v_group[:, :, :, :, D:D + 1], 1.0)
            nc.gpsimd.memset(v_group[:, :, :, :, D + 1:], 0.0)
            values(0, 0)
            values(1, 1)
            if not decayed:
                for stack in s_stack + t_stack[0] + t_stack[1]:
                    last = nc.gpsimd.memset(stack[:, 1].rearrange("p h t -> p (h t)").bitcast(U32), 0)
                last.then_inc(zeroed, 1)
                for b in range(2):
                    pool.wait_ge(zeroed, b + 1)
                    pool_ones(nc, t_stack[b][1], 1).then_inc(zeroed, 1)
                pool.wait_ge(zeroed, 3)
                nc.gpsimd.tensor_tensor(x_tok[:, :, :], x_tok[:, :, :],
                                        w["bo"][:, :].rearrange("p (o c) -> p o c", o=1).broadcast_to([P, NT, C]),
                                        ALU.add)
            with pool.Fori(1, NG - 2, 2) as i:
                pool.wait_ge(pv_done, i * NS)
                values(i + 1, 0)
                pool.wait_ge(pv_done, (i + 1) * NS)
                values(i + 2, 1)

        @block.vector
        def _(dve):
            dve.wait_ge(later_loaded, 16 * n_later)
            if not decayed:
                nc.vector.memset(half_max[:, :, :, :], -3e38).then_inc(preset, 1)
                dve.wait_ge(preset, 1)

            def work(order, n, parity, base, chain, target):
                k = 0
                for kind, a, b in order:
                    if kind not in ("S", "MT", "ON"):
                        continue
                    at = bank((parity + k) % 2)
                    dve.wait_ge(slot_full, base + (k + 1))
                    if kind == "S" and units[a][2][5] is not None:
                        nc.vector.memset(spare[:, a % 2:a % 2 + 1], 0.0)
                    k += 1
                    if kind == "S":
                        h0, heads, i, half, width, diag = units[a][2]
                        if diag is not None:
                            nc.vector.tensor_tensor_reduce(
                                out=junk[:, a % 2, :], in0=at, in1=diagonal[:, 3 * P - diag:3 * P - diag + BANK], scale=1.0,
                                scalar=-3e38, op0=ALU.mult, op1=ALU.max,
                                accum_out=half_max[:, h0, i, half:half + 1]).then_inc(slot_free, 1)
                        else:
                            nc.vector.tensor_reduce(
                                half_max[:, h0:h0 + heads, i, half],
                                at[:, 0:heads * width].rearrange("p (h w) -> p h w", w=width), AX.X, ALU.max)\
                                .then_inc(slot_free, 1)
                        if a == NU - 1:
                            dve.wait_ge(slot_free, base + k)
                            nc.vector.tensor_reduce(
                                row_max[:, :, :], half_max[:, :, :, :].rearrange("p h k (m x) -> p m (h k) x", m=1)
                                .broadcast_to([P, 3, MR, 2]), AX.X, ALU.max)\
                                .then_inc(max_ready, 1)
                    elif kind == "MT":
                        src = at[0:3 * MR, 0:P]
                        if not (type(target) is int and target == 0):
                            dve.wait_ge(m_loaded, target * (16 * NV))
                        nc.vector.tensor_scalar(max_parts[:, :], src, -1.0, None, ALU.mult).then_inc(vector_done, 1)
                        dve.wait_ge(vector_done, chain + 1)
                        nc.vector.scalar_tensor_tensor(out=max_rest[:, :], in0=src, scalar=-1.0,
                                                       in1=max_parts[:, :], op0=ALU.mult, op1=ALU.subtract)\
                            .then_inc(slot_free, 1)
                        dve.wait_ge(slot_free, base + k)
                        second, third = slice(MR, 2 * MR), slice(2 * MR, 3 * MR)
                        nc.vector.tensor_copy(max_parts[second, :], max_rest[second, :]).then_inc(vector_done, 1)
                        nc.vector.tensor_copy(max_second[third, :], max_rest[third, :]).then_inc(vector_done, 1)
                        chain = chain + 3
                        dve.wait_ge(vector_done, chain)
                        nc.vector.tensor_tensor(max_parts[third, :], max_rest[third, :], max_second[third, :],
                                                ALU.subtract).then_inc(parts_ready, 1)
                    else:
                        view = at.rearrange("p (k h m) -> p k h m", k=4, h=HG)
                        nc.vector.reciprocal(inverse[:, a, :, :], view[:, :, :, D]).then_inc(vector_done, 1)
                        chain = chain + 1
                        dve.wait_ge(vector_done, chain)
                        dst = attn_tok[:, 4 * a:4 * a + 4, bass.ds(n - 1, 1), :, :]
                        nc.vector.tensor_tensor(
                            dst.rearrange("p k o h d -> p (k o) h d"), view[:, :, :, 0:D],
                            inverse[:, a, :, :].rearrange("p k (h o) -> p k h o", o=1).broadcast_to([P, 4, HG, D]),
                            ALU.mult).then_inc(slot_free, 1)

            def body(n, par):
                work(order_of(n), n, slots_before(n if type(n) is int else 2 - par) % 2, slots_before(n),
                     chain_before(n), n + 1)
            work(prologue, 0, 0, 0, 0, 0)
            iterations(dve, body)
            work(closing, NG, (slots_before(NG - 1) + 2) % 2, slots_before(NG - 1) + 2, chain_before(NG - 1) + 2, 0)


def route_phase(nc, sem, sb, ins, w, parts, comb, w32, pick, bank):
    SG, SE = 8 - TOPG, 8 - TOPK
    BIG = 1e30
    gate, bias, ident = w["gate"], w["gate_bias"], w["ident"]
    score = sb("score", [P, NT, E], F32)
    best = sb("best", [P, NT, GROUPS + SG], F32)
    best_left = sb("best_left", [P, NT, GROUPS + SG], F32)
    chosen = sb("chosen", [P, NT, GROUPS], F32)
    masked = sb("masked", [P, NT, E + SE], F32)
    left = sb("left", [P, NT, E + SE], F32)
    top = sb("top", [P, 2, NT, 8], F32)
    total = sb("total", [P, 2, NT], F32)
    rest = sb("rest", [E, TOK], F32)
    with ExitStack() as c:
        w_loaded, pick_loaded = ([c.enter_context(sem(f"{s}_loaded{b}")) for b in range(2)] for s in ("w", "pick"))
        sigmoids, step, weights_ready, turned, first_ready, rest_ready, second_ready, third_ready, \
            moved, filled = (c.enter_context(sem(s)) for s in (
                "sigmoids", "step", "weights_ready", "turned", "first_ready", "rest_ready",
                "second_ready", "third_ready", "moved", "filled"))
        block = c.enter_context(nc.Block())
        per = BANK // E

        def load(sp, p, par):
            sp.dma_start(w32[:, par, :], ins["experts"][bass.ds(p, 1)].rearrange("o p n -> (o p) n"))\
                .then_inc(w_loaded[par], 16)

        def load_pick(sp, p, par):
            sp.dma_start(pick[:, par, :], ins["pick"][bass.ds(p, 1)].rearrange("o r m -> (o r) m"))\
                .then_inc(pick_loaded[par], 16)

        @block.sync
        def _(sp):
            for p in range(2):
                load(sp, p, p)
                load_pick(sp, p, p)
            for p, ready in enumerate((first_ready, second_ready, third_ready)):
                sp.wait_ge(ready, CH)
                for half in range(2):
                    sp.dma_start(comb[32 * p:32 * p + 32, half, :], parts[32 * half:32 * half + 32, p, :])\
                        .then_inc(moved, 16)

        @block.tensor
        def _(pe):
            pe.wait_ge(weights_ready, 1)
            for t in range(NT):
                nc.tensor.transpose(bank(4 + t // 4)[0:E, t % 4 * P:(t % 4 + 1) * P], score[:, t, :], ident[:, :])\
                    .then_inc(turned, 1)

        @block.gpsimd
        def _(pool):
            nc.gpsimd.memset(best[:, :, GROUPS:], BIG).then_inc(filled, 1)
            nc.gpsimd.memset(masked[:, :, E:], BIG).then_inc(filled, 1)
            for k in range(CH):
                chunk = slice(k * BANK, (k + 1) * BANK)
                pool.wait_ge(second_ready, k + 1)
                nc.gpsimd.tensor_tensor(parts[:, 2, chunk], rest[:, chunk], parts[:, 1, chunk], ALU.subtract)\
                    .then_inc(third_ready, 1)

        @block.scalar
        def _(act):
            for k in range(NT // per):
                nc.scalar.activation(score[:, per * k:per * (k + 1), :].rearrange("p t e -> p (t e)"), bank(k),
                                     ACT.Sigmoid).then_inc(sigmoids, 1)
            for k in range(CH):
                chunk = slice(k * BANK, (k + 1) * BANK)
                act.wait_ge(turned, 4 * (k + 1))
                nc.scalar.activation(parts[:, 0, chunk], bank(4 + k)[0:E, :], ACT.Copy).then_inc(first_ready, 1)
            for k in range(CH):
                chunk = slice(k * BANK, (k + 1) * BANK)
                act.wait_ge(rest_ready, k + 1)
                nc.scalar.activation(parts[:, 1, chunk], rest[:, chunk], ACT.Copy).then_inc(second_ready, 1)

        @block.vector
        def _(dve):
            n = [0]

            def link(ins_):
                n[0] += 1
                ins_.then_inc(step, 1)
                dve.wait_ge(step, n[0])

            dve.wait_ge(sigmoids, NT // per)
            link(nc.vector.tensor_tensor(score[:, :, :], score[:, :, :],
                                         bias[:, :].rearrange("p (o e) -> p o e", o=1).broadcast_to([P, NT, E]),
                                         ALU.add))
            dve.wait_ge(filled, 2)
            link(nc.vector.tensor_reduce(best[:, :, 0:GROUPS],
                                         score[:, :, :].rearrange("p t (g e) -> p t g e", g=GROUPS), AX.X, ALU.max))
            for t in range(NT):
                last = nc.vector.max(top[:, 0, t, :], best[:, t, :])
            link(last)
            for t in range(NT):
                last = nc.vector.match_replace(best_left[:, t, :], top[:, 0, t, :], best[:, t, :], -BIG)
            link(last)
            link(nc.vector.tensor_tensor(chosen[:, :, :], best_left[:, :, 0:GROUPS], best[:, :, 0:GROUPS],
                                         ALU.not_equal))
            for g in range(GROUPS):
                e = E // GROUPS
                last = nc.vector.tensor_tensor(
                    masked[:, :, g * e:(g + 1) * e], score[:, :, g * e:(g + 1) * e],
                    chosen[:, :, g:g + 1].broadcast_to([P, NT, e]), ALU.mult)
            link(last)
            for t in range(NT):
                last = nc.vector.max(top[:, 1, t, :], masked[:, t, :])
            link(last)
            for t in range(NT):
                last = nc.vector.match_replace(left[:, t, :], top[:, 1, t, :], masked[:, t, :], -BIG)
            link(last)
            link(nc.vector.tensor_tensor(score[:, :, :], left[:, :, 0:E], masked[:, :, 0:E], ALU.not_equal))
            link(nc.vector.tensor_tensor(score[:, :, :], score[:, :, :], masked[:, :, 0:E], ALU.mult))
            link(nc.vector.tensor_reduce(total[:, 0, :], score[:, :, :], AX.X, ALU.add))
            link(nc.vector.tensor_scalar(total[:, 1, :], total[:, 0, :], 1e-8, None, ALU.add))
            link(nc.vector.reciprocal(total[:, 0, :], total[:, 1, :]))
            link(nc.vector.tensor_scalar(total[:, 1, :], total[:, 0, :], HS, None, ALU.mult))
            nc.vector.tensor_tensor(score[:, :, :], score[:, :, :],
                                    total[:, 1, :].rearrange("p (t o) -> p t o", o=1).broadcast_to([P, NT, E]),
                                    ALU.mult).then_inc(weights_ready, 1)
            for k in range(CH):
                chunk = slice(k * BANK, (k + 1) * BANK)
                dve.wait_ge(first_ready, k + 1)
                nc.vector.tensor_tensor(rest[:, chunk], bank(4 + k)[0:E, :], parts[:, 0, chunk], ALU.subtract)\
                    .then_inc(rest_ready, 1)
    return load, load_pick, w_loaded, pick_loaded, moved


def expert_phase(nc, sem, sb, ins, loader, xh, xl, comb, w32, pick, x_tok, ident, bank, out):
    NP = PAIRS + 1
    load, load_pick, w_loaded, pick_loaded, moved = loader
    wh = sb("wh", [P, 2, 3 * P], F16)
    wl = sb("wl", [P, 2, 3 * P], F16)
    act_g = sb("act_g", [P, 2, BANK], F32)
    gated = sb("gated", [P, 2, BANK], F32)
    hidden = sb("hidden", [P, 2, BANK], F32)
    hh = sb("hh", [P, CH, BANK], F16)
    hl = sb("hl", [P, CH, BANK], F16)
    yT = sb("yT", [P, TOK], F32)
    LAG = 2
    SPLIT = 1
    UPPER, DOWN = slice(0, 2 * P), slice(2 * P, 3 * P)
    ACC, GATE, UP, WEIGHT = 0, 4, 5, 6
    with ExitStack() as c:
        (upper_high, upper_low, down_high, down_low, gate_ps, up_ps, weight_ps, silu_done, gated_done,
         hidden_done, high_done, low_done, down_done, y_ready, turned, added, stored) = (
            c.enter_context(sem(s)) for s in (
                "upper_high", "upper_low", "down_high", "down_low", "gate_ps", "up_ps", "weight_ps",
                "silu_done", "gated_done", "hidden_done", "high_done", "low_done", "down_done", "y_ready", "turned",
                "added", "stored"))
        block = c.enter_context(nc.Block())

        def number(p, k):
            return p * CH + k

        @block.sync
        def _(sp):
            with sp.Fori(2, PAIRS, 2) as i:
                for par in range(2):
                    sp.wait_ge(down_low, i + (par - 1))
                    load(sp, i + par, par)
                    sp.wait_ge(weight_ps, (i + (par - 1)) * CH)
                    load_pick(sp, i + par, par)
            sp.wait_ge(down_low, PAIRS - 1)
            load(sp, PAIRS, 0)
            if out is not None:
                o = out.rearrange("(t p) c -> p t c", p=P)
                for k in range(CH):
                    sp.wait_ge(added, k + 1)
                    sp.dma_start(o[:, 4 * k:4 * k + 4, :], x_tok[:, 4 * k:4 * k + 4, :]).then_inc(stored, 16)
                sp.wait_ge(stored, 16 * CH)

        @block.tensor
        def _(pe):
            def product(dst, par, m, high, low, first, last):
                w = slice(m * P, (m + 1) * P)
                nc.tensor.matmul(dst, wh[:, par, w], low, start=first, stop=False)
                nc.tensor.matmul(dst, wl[:, par, w], high, start=False, stop=False)
                return nc.tensor.matmul(dst, wh[:, par, w], high, start=False, stop=last)

            def pair(p, par, half):
                first = type(p) is int and p == 0
                shared = half is None
                pe.wait_ge(upper_low, p + 1)
                for k in range(CH):
                    chunk = slice(k * BANK, (k + 1) * BANK)
                    if not (first and k == 0):
                        pe.wait_ge(silu_done, number(p, k))
                    product(bank(GATE), par, 0, xh[:, chunk], xl[:, chunk], True, True).then_inc(gate_ps, 1)
                    if not (first and k == 0):
                        pe.wait_ge(hidden_done if shared and k else gated_done, number(p, k))
                    product(bank(UP), par, 1, xh[:, chunk], xl[:, chunk], True, True).then_inc(up_ps, 1)
                    if not shared:
                        if k == 0:
                            pe.wait_ge(pick_loaded[par], (p + (2 - par)) * 8)
                        if k == 0 and first:
                            pe.wait_ge(moved, 6 * 16)
                        if not (first and k == 0):
                            pe.wait_ge(hidden_done, number(p, k))
                        nc.tensor.matmul(bank(WEIGHT), pick[:, par, :], comb[:, half, chunk], start=True, stop=True)\
                            .then_inc(weight_ps, 1)
                    if not (first and k < LAG):
                        at = (k - LAG) % CH
                        of = par if k >= LAG else 1 - par
                        begins = type(p) is int and (p == 0 or (p == 1 and k < LAG))
                        if k == LAG:
                            pe.wait_ge(down_low, p + 1)
                        pe.wait_ge(low_done, number(p, k - LAG + 1))
                        product(bank(ACC + at), of, 2, hh[:, at, :], hl[:, at, :], begins,
                                shared and k >= LAG).then_inc(down_done, 1)

            pair(0, 0, 0)
            pair(1, 1, 0)
            for half in range(2):
                with pe.Fori(2 if half == 0 else PAIRS // 2, PAIRS // (2 - half), 2) as i:
                    pair(i, 0, half)
                    pair(i + 1, 1, half)
            pair(PAIRS, 0, None)
            for at in range(CH - LAG, CH):
                pe.wait_ge(low_done, number(PAIRS, at + 1))
                product(bank(ACC + at), 0, 2, hh[:, at, :], hl[:, at, :], False, True).then_inc(down_done, 1)
            for t in range(NT):
                pe.wait_ge(y_ready, t // 4 + 1)
                nc.tensor.transpose(bank(4 + t // 4)[:, t % 4 * P:(t % 4 + 1) * P], yT[:, t * P:(t + 1) * P],
                                    ident[:, :]).then_inc(turned, 1)

        @block.scalar
        def _(act):
            def high(p, k):
                act.wait_ge(hidden_done, number(p, k + 1))
                if not (type(p) is int and p == 0):
                    act.wait_ge(down_done, number(p, k + 1) - CH)
                nc.scalar.activation(hh[:, k, :], hidden[:, k % 2, :], ACT.Copy).then_inc(high_done, 1)

            def pair(p, shared=False):
                first = type(p) is int and p == 0
                for k in range(CH):
                    act.wait_ge(gate_ps, number(p, k + 1))
                    if not (first and k < 2):
                        act.wait_ge(hidden_done if shared and k >= 2 else gated_done, number(p, k - 1))
                    nc.scalar.activation(act_g[:, k % 2, :], bank(GATE), ACT.Silu, scale=1.0 / (XS * WS))\
                        .then_inc(silu_done, 1)
                    if k >= 1:
                        high(p, k - 1)
                    elif not first:
                        high(p - 1, CH - 1)
            pair(0)
            pair(1)
            with act.Fori(2, PAIRS, 2) as i:
                pair(i)
                pair(i + 1)
            pair(PAIRS, shared=True)
            high(PAIRS, CH - 1)
            for k in range(CH):
                act.wait_ge(down_done, number(PAIRS, k + 1))
                nc.scalar.activation(yT[:, k * BANK:(k + 1) * BANK], bank(ACC + k), ACT.Copy,
                                     scale=1.0 / (HS * WS)).then_inc(y_ready, 1)

        @block.vector
        def _(dve):
            def split(p, par, part, high, low):
                nc.vector.tensor_scalar(wh[:, par, part], w32[:, par, part], WS, None, ALU.mult).then_inc(high, 1)
                dve.wait_ge(high, p + 1)
                nc.vector.scalar_tensor_tensor(out=wl[:, par, part], in0=w32[:, par, part], scalar=WS,
                                               in1=wh[:, par, part], op0=ALU.mult, op1=ALU.subtract)\
                    .then_inc(low, 1)

            def split_upper(p, par, first=False):
                dve.wait_ge(w_loaded[par], (p + (2 - par)) * 8)
                if not first:
                    dve.wait_ge(up_ps, number(p - 1, 0))
                split(p, par, UPPER, upper_high, upper_low)

            def split_down(p, par, first=False):
                if not first:
                    dve.wait_ge(down_done, number(p - 1, 0))
                split(p, par, DOWN, down_high, down_low)

            def pair(p, par, shared=False):
                first = type(p) is int and p == 0
                for k in range(CH):
                    dve.wait_ge(up_ps, number(p, k + 1))
                    dve.wait_ge(silu_done, number(p, k + 1))
                    if not (first and k < 2):
                        dve.wait_ge(low_done, number(p, k - 1))
                    target = hidden if shared else gated
                    done = nc.vector.scalar_tensor_tensor(
                        out=target[:, k % 2, :], in0=bank(UP), scalar=(HS if shared else 1.0) / (XS * WS),
                        in1=act_g[:, k % 2, :], op0=ALU.mult, op1=ALU.mult)
                    if shared:
                        done.then_inc(hidden_done, 1)
                    else:
                        done.then_inc(gated_done, 1)
                        dve.wait_ge(gated_done, number(p, k + 1))
                        dve.wait_ge(weight_ps, number(p, k + 1))
                        nc.vector.tensor_tensor(hidden[:, k % 2, :], bank(WEIGHT), gated[:, k % 2, :], ALU.mult)\
                            .then_inc(hidden_done, 1)
                    if k == SPLIT and not shared:
                        split_upper(p + 1, 1 - par, first)
                    elif k == SPLIT + 1 and not shared:
                        split_down(p + 1, 1 - par, first)

            split_upper(0, 0, True)
            split_down(0, 0, True)
            pair(0, 0)
            pair(1, 1)
            with dve.Fori(2, PAIRS, 2) as i:
                pair(i, 0)
                pair(i + 1, 1)
            pair(PAIRS, 0, shared=True)
            flat = x_tok[:, :, :].rearrange("p t c -> p (t c)")
            for k in range(CH):
                dve.wait_ge(turned, 4 * (k + 1))
                part = flat[:, k * BANK:(k + 1) * BANK]
                nc.vector.tensor_tensor(part, part, bank(4 + k), ALU.add).then_inc(added, 1)

        @block.gpsimd
        def _(pool):
            def pair(p):
                for k in range(CH):
                    pool.wait_ge(high_done, number(p, k + 1))
                    nc.gpsimd.tensor_tensor(hl[:, k, :], hidden[:, k % 2, :], hh[:, k, :], ALU.subtract)\
                        .then_inc(low_done, 1)
            pair(0)
            pair(1)
            with pool.Fori(2, PAIRS, 2) as i:
                pair(i)
                pair(i + 1)
            pair(PAIRS)


def kernel(**inputs):
    import ml_dtypes
    import numpy as np
    import concourse.bacc as bacc
    from concourse.bass_utils import run_bass_kernel_spmd

    def get(n):
        return np.asarray(inputs[n])

    bf16 = ml_dtypes.bfloat16
    arrays = {"x": get("L0_attn_a_x").reshape(TOK, C)}
    for key, n in (("wkd", "Wkd"), ("bkd", "bkd"), ("wo", "Wo"), ("bo", "bo")):
        arrays[key] = get("L0_attn_a_" + n)

    def by_group(a):
        return a.reshape(a.shape[:-1] + (HG, HG, D)).swapaxes(-1, -2).reshape(a.shape)
    arrays["wq"], arrays["bq"] = by_group(get("L0_attn_a_Wq")), by_group(get("L0_attn_a_bq"))
    wku, bku = get("L0_attn_a_Wku"), get("L0_attn_a_bku")
    arrays["wk_low"] = by_group(np.concatenate([wku[:, :C], wku[:, :C]]))
    arrays["wv_low"] = np.concatenate([wku[:, C:], wku[:, C:]])
    arrays["bk"], arrays["bv"] = by_group(bku[:C]), bku[C:]
    for key, n in (("b_wk", "W_k"), ("b_wv", "W_v"), ("b_wo", "W_o"), ("b_wd", "W_down_kv"), ("b_wuv", "W_up_v")):
        arrays[key] = get("L0_attn_b_" + n)
    arrays["b_wq"], arrays["b_wuk"] = by_group(get("L0_attn_b_W_q")), by_group(get("L0_attn_b_W_up_k"))
    arrays["gate_w"] = get("L0_ffn_gate_w").T
    arrays["gate_bias"] = get("L0_ffn_gate_bias")
    def up(w, s):
        return np.concatenate([get(w).reshape(PAIRS, P, C), get(s)[None]]).transpose(0, 2, 1)
    down = np.concatenate([get("L0_ffn_ed_w").transpose(0, 2, 1).reshape(PAIRS, P, C), get("L0_ffn_sd_w").T[None]])
    arrays["experts"] = np.concatenate([up("L0_ffn_eg_w", "L0_ffn_sg_w"), up("L0_ffn_eu_w", "L0_ffn_su_w"), down], 2)
    eye = np.eye(P, dtype=np.float32)
    arrays["ident"], arrays["ident_b"] = eye, eye.astype(bf16)
    at = np.arange(P)
    above = (at[None, :] > at[:, None]) * np.float32(-1e30)
    arrays["mask"] = np.stack([above, above.T, (at[:, None] <= at[None, :]) * np.float32(-1e30)]).astype(bf16)
    t = np.arange(T, dtype=np.float64)
    arrays["decay"] = np.exp(np.stack([-0.01 * t, 0.01 * t])).astype(np.float32)
    diagonal = np.ones((P, 7 * P), np.float32)
    diagonal[:, 3 * P:4 * P] = np.exp(-0.02 * np.maximum(0, at[None, :] - at[:, None]))
    arrays["diagonal"] = diagonal
    row, col, pair = np.arange(96)[None, :, None], np.arange(P)[None, None, :], np.arange(PAIRS + 1)[:, None, None]
    arrays["pick"] = (row % 32 == 2 * (pair % (PAIRS // 2)) + col // I).astype(bf16)

    nc = bacc.Bacc("TRN2", target_bir_lowering=False, num_devices=1)
    feed, ins = {}, {}
    for key, a in arrays.items():
        a = np.ascontiguousarray(a)
        feed[f"in_{key}"] = a
        ins[key] = nc.dram_tensor(f"in_{key}", a.shape, mybir.dt.from_np(a.dtype), kind="ExternalInput").ap()
    out = nc.dram_tensor("out_0", (TOK, C), F32, kind="ExternalOutput").ap()
    kernel_program(nc, ins, out)
    r = run_bass_kernel_spmd(nc, [feed], core_ids=[0])
    return r.results[0]["out_0"].reshape(B, T, C)
```
